# Optimizing a Trainium2 kernel written in Bass

```python
import numpy as np
import jax
import jax.numpy as jnp

def _softmax(x, axis=-1):
    return jax.nn.softmax(x, axis=axis)

def _gelu(x):
    return jax.nn.gelu(x, approximate=True)

def _silu(x):
    return jax.nn.silu(x)

def _sigmoid(x):
    return jax.nn.sigmoid(x)

def _layernorm(x, axis=-1, eps=1e-05):
    m = jnp.mean(x, axis=axis, keepdims=True)
    v = jnp.var(x, axis=axis, keepdims=True)
    return (x - m) / jnp.sqrt(v + eps)

def _scatter_add(tgt, idx, src, axis=0):
    return tgt.at[idx].add(src)

def _segment_sum(src, seg, n):
    return jax.ops.segment_sum(src, seg, n)
kernel_name = 'mk_prb_d1_jaxref_r4_bb15a5'

def setup_inputs(seed: int=0):
    np.random.seed(seed)
    _w = jnp.asarray

    def _L0_attn_setup():
        import jax, jax.numpy as jnp
        import numpy as np
        B, S, D = (2, 512, 256)
        H, DH = (16, 64)
        DQL, DKVL = (128, 128)
        DR = 64
        TOPK = 64
        LN_EPS = 1e-05
        ROPE_BASE = 10000.0

        def _rope_tables(seq_len, dim):
            inv_freq = 1.0 / ROPE_BASE ** (np.arange(0, dim, 2, dtype=np.float32) / dim)
            t = np.arange(seq_len, dtype=np.float32)
            freqs = np.outer(t, inv_freq)
            cos = np.concatenate([np.cos(freqs), np.cos(freqs)], -1)[:, ::2]
            sin = np.concatenate([np.sin(freqs), np.sin(freqs)], -1)[:, ::2]
            return (jnp.asarray(cos), jnp.asarray(sin))

        def _apply_rope_subspace(x, d_rope):
            s = x.shape[-2]
            cos, sin = _rope_tables(s, d_rope)
            xr, xp = (x[..., :d_rope], x[..., d_rope:])
            e, o = (xr[..., 0::2], xr[..., 1::2])
            rot = jnp.stack([e * cos - o * sin, e * sin + o * cos], axis=-1).reshape(xr.shape)
            return jnp.concatenate([rot, xp], axis=-1)

        def _reference_tuple_inner(x, w_down_q, w_down_kv, w_up_q, w_up_k, w_up_v, w_out, ln_scale, ln_bias):
            b, s, d = x.shape
            residual = x
            mu = jnp.mean(x, axis=-1, keepdims=True)
            var = jnp.mean((x - mu) ** 2, axis=-1, keepdims=True)
            h = (x - mu) * jax.lax.rsqrt(var + LN_EPS) * ln_scale + ln_bias
            c_q = h @ w_down_q.T
            c_kv = h @ w_down_kv.T
            q = (c_q @ w_up_q.T).reshape(b, s, H, DH).transpose(0, 2, 1, 3)
            k = (c_kv @ w_up_k.T).reshape(b, s, H, DH).transpose(0, 2, 1, 3)
            v = (c_kv @ w_up_v.T).reshape(b, s, H, DH).transpose(0, 2, 1, 3)
            q = _apply_rope_subspace(q, DR)
            k = _apply_rope_subspace(k, DR)
            scale = 1.0 / np.sqrt(DH).astype(np.float32)
            scores = jnp.einsum('bhqd,bhkd->bhqk', q, k) * scale
            _, indices = jax.lax.top_k(scores, min(TOPK, s))
            attn = jax.nn.softmax(scores, axis=-1)
            out = jnp.einsum('bhqk,bhkd->bhqd', attn, v)
            out = out.transpose(0, 2, 1, 3).reshape(b, s, H * DH)
            out = out @ w_out.T + residual
            return (out, indices.astype(jnp.int64))
        key = jax.random.key(seed)
        ks = jax.random.split(key, 7)
        init = lambda k, shape: jax.random.normal(k, shape, jnp.float32) * 0.02
        return {'x': jax.random.normal(ks[0], (B, S, D), jnp.float32), 'w_down_q': init(ks[1], (DQL, D)), 'w_down_kv': init(ks[2], (DKVL, D)), 'w_up_q': init(ks[3], (H * DH, DQL)), 'w_up_k': init(ks[4], (H * DH, DKVL)), 'w_up_v': init(ks[5], (H * DH, DKVL)), 'w_out': init(ks[6], (D, H * DH)), 'ln_scale': jnp.ones((D,), jnp.float32), 'ln_bias': jnp.zeros((D,), jnp.float32)}
    _L0_attn_in = _L0_attn_setup()

    def _L0_ffn_setup():
        import jax, jax.numpy as jnp
        import numpy as np
        TOP_K = 2
        key = jax.random.key(seed)
        k1, k2, k3, k4 = jax.random.split(key, 4)
        B, S, H, E, F = (2, 256, 256, 16, 256)
        hidden_states = jax.random.normal(k1, (B, S, H), dtype=jnp.float32)
        router_w = jax.random.normal(k2, (H, E), dtype=jnp.float32) * 0.02
        w_gate_up = jax.random.normal(k3, (E, H, 2 * F), dtype=jnp.float32) * 0.02
        w_down = jax.random.normal(k4, (E, F, H), dtype=jnp.float32) * 0.02
        return {'hidden_states': hidden_states, 'router_w': router_w, 'w_gate_up': w_gate_up, 'w_down': w_down}
    _L0_ffn_in = _L0_ffn_setup()
    _d = {'L0_attn_x': _L0_attn_in['x'], 'L0_attn_w_down_q': _L0_attn_in['w_down_q'], 'L0_attn_w_down_kv': _L0_attn_in['w_down_kv'], 'L0_attn_w_up_q': _L0_attn_in['w_up_q'], 'L0_attn_w_up_k': _L0_attn_in['w_up_k'], 'L0_attn_w_up_v': _L0_attn_in['w_up_v'], 'L0_attn_w_out': _L0_attn_in['w_out'], 'L0_attn_ln_scale': _L0_attn_in['ln_scale'], 'L0_attn_ln_bias': _L0_attn_in['ln_bias'], 'L0_ffn_router_w': _L0_ffn_in['router_w'], 'L0_ffn_w_gate_up': _L0_ffn_in['w_gate_up'], 'L0_ffn_w_down': _L0_ffn_in['w_down']}
    _x0 = _d['L0_attn_x']
    _d['L0_attn_x'] = jax.random.normal(jax.random.fold_in(jax.random.key(seed), 1), (2, 2048, 256), dtype=_x0.dtype)
    del _x0
    return _d

def reference(L0_attn_x, L0_attn_w_down_q, L0_attn_w_down_kv, L0_attn_w_up_q, L0_attn_w_up_k, L0_attn_w_up_v, L0_attn_w_out, L0_attn_ln_scale, L0_attn_ln_bias, L0_ffn_router_w, L0_ffn_w_gate_up, L0_ffn_w_down):

    def _L0_attn_ref(x, w_down_q, w_down_kv, w_up_q, w_up_k, w_up_v, w_out, ln_scale, ln_bias):
        import jax, jax.numpy as jnp
        import numpy as np
        B, S, D = (2, 512, 256)
        H, DH = (16, 64)
        DQL, DKVL = (128, 128)
        DR = 64
        TOPK = 64
        LN_EPS = 1e-05
        ROPE_BASE = 10000.0

        def _rope_tables(seq_len, dim):
            inv_freq = 1.0 / ROPE_BASE ** (np.arange(0, dim, 2, dtype=np.float32) / dim)
            t = np.arange(seq_len, dtype=np.float32)
            freqs = np.outer(t, inv_freq)
            cos = np.concatenate([np.cos(freqs), np.cos(freqs)], -1)[:, ::2]
            sin = np.concatenate([np.sin(freqs), np.sin(freqs)], -1)[:, ::2]
            return (jnp.asarray(cos), jnp.asarray(sin))

        def _apply_rope_subspace(x, d_rope):
            s = x.shape[-2]
            cos, sin = _rope_tables(s, d_rope)
            xr, xp = (x[..., :d_rope], x[..., d_rope:])
            e, o = (xr[..., 0::2], xr[..., 1::2])
            rot = jnp.stack([e * cos - o * sin, e * sin + o * cos], axis=-1).reshape(xr.shape)
            return jnp.concatenate([rot, xp], axis=-1)

        def _reference_tuple_inner(x, w_down_q, w_down_kv, w_up_q, w_up_k, w_up_v, w_out, ln_scale, ln_bias):
            b, s, d = x.shape
            residual = x
            mu = jnp.mean(x, axis=-1, keepdims=True)
            var = jnp.mean((x - mu) ** 2, axis=-1, keepdims=True)
            h = (x - mu) * jax.lax.rsqrt(var + LN_EPS) * ln_scale + ln_bias
            c_q = h @ w_down_q.T
            c_kv = h @ w_down_kv.T
            q = (c_q @ w_up_q.T).reshape(b, s, H, DH).transpose(0, 2, 1, 3)
            k = (c_kv @ w_up_k.T).reshape(b, s, H, DH).transpose(0, 2, 1, 3)
            v = (c_kv @ w_up_v.T).reshape(b, s, H, DH).transpose(0, 2, 1, 3)
            q = _apply_rope_subspace(q, DR)
            k = _apply_rope_subspace(k, DR)
            scale = 1.0 / np.sqrt(DH).astype(np.float32)
            scores = jnp.einsum('bhqd,bhkd->bhqk', q, k) * scale
            _, indices = jax.lax.top_k(scores, min(TOPK, s))
            attn = jax.nn.softmax(scores, axis=-1)
            out = jnp.einsum('bhqk,bhkd->bhqd', attn, v)
            out = out.transpose(0, 2, 1, 3).reshape(b, s, H * DH)
            out = out @ w_out.T + residual
            return (out, indices.astype(jnp.int64))
        return _reference_tuple_inner(x, w_down_q, w_down_kv, w_up_q, w_up_k, w_up_v, w_out, ln_scale, ln_bias)[0]

    def _L0_ffn_ref(hidden_states, router_w, w_gate_up, w_down):
        import jax, jax.numpy as jnp
        import numpy as np
        TOP_K = 2
        B, S, H = hidden_states.shape
        E = router_w.shape[-1]
        flat = hidden_states.reshape(-1, H)
        T = flat.shape[0]
        logits = flat @ router_w
        top_vals, top_idx = jax.lax.top_k(logits, TOP_K)
        routing_weights = jax.nn.softmax(top_vals, axis=-1)
        combine = jnp.zeros((T, E), dtype=flat.dtype)
        combine = combine.at[jnp.arange(T)[:, None], top_idx].add(routing_weights)
        gu = jnp.einsum('th,ehf->etf', flat, w_gate_up)
        gate, up = jnp.split(gu, 2, axis=-1)
        gated = jax.nn.silu(gate) * up
        expert_out = jnp.einsum('etf,efh->eth', gated, w_down)
        out = jnp.einsum('eth,te->th', expert_out, combine)
        return out.reshape(B, S, H)
    x = L0_attn_x
    xn = _layernorm(x, axis=-1)
    x = x + _L0_attn_ref(xn, L0_attn_w_down_q, L0_attn_w_down_kv, L0_attn_w_up_q, L0_attn_w_up_k, L0_attn_w_up_v, L0_attn_w_out, L0_attn_ln_scale, L0_attn_ln_bias) + _L0_ffn_ref(xn, L0_ffn_router_w, L0_ffn_w_gate_up, L0_ffn_w_down)
    return x

_drawn_inputs = setup_inputs


def setup_inputs(seed=0):
    import zlib

    import numpy as np

    out = dict(_drawn_inputs(seed))
    spreads = {'L0_attn_ln_scale': (1.0, 0.6), 'L0_attn_ln_bias': (0.0, 0.8)}
    factors = {'L0_attn_w_down_q': 8.0,
     'L0_attn_w_down_kv': 8.0,
     'L0_attn_w_up_q': 8.0,
     'L0_attn_w_up_k': 8.0,
     'L0_attn_w_up_v': 8.0,
     'L0_attn_w_out': 8.0,
     'L0_ffn_router_w': 8.0,
     'L0_ffn_w_gate_up': 8.0,
     'L0_ffn_w_down': 8.0}
    for name, (base, spread) in spreads.items():
        noise = np.random.default_rng([zlib.crc32(name.encode()), seed]).standard_normal(out[name].shape)
        drawn = base * np.exp(spread * noise) if base else spread * noise
        out[name] = jnp.asarray(drawn.astype(out[name].dtype))
    for name, factor in factors.items():
        out[name] = (out[name] * factor).astype(out[name].dtype)
    return out
```

```python
from contextlib import ExitStack

import concourse.bass as bass
import numpy as np
from concourse import mybir

ALU = mybir.AluOpType
ACT = mybir.ActivationFunctionType
AX = mybir.AxisListType
F32 = mybir.dt.float32
F32R = mybir.dt.float32r
U32 = mybir.dt.uint32

P = 128
B, S, D = 2, 2048, 256
H, DH = 16, 64
E, F = 16, 256
LATENT = 128
TOKENS = B * S
TILES = TOKENS // P
CH = 512
CT = CH // P
KD = D // P
KT = S // P
QC = S // CH
EPS = 1e-5
SCALE = 1.0 / 8.0
PAIRS = B * H // 2
CHOICES = 2
SLOT_TILES = 80
assert SLOT_TILES >= CHOICES * TOKENS // P + E - 1


def need(eng, semaphore, value):
    if isinstance(value, int) and value <= 0:
        return
    eng.wait_ge(semaphore, value)


def within(n, total):
    return not isinstance(n, int) or 0 <= n < total


class Memory:

    def __init__(self, nc, ctx):
        self.nc, self.ctx = nc, ctx

    def sb(self, name, shape, dtype=F32):
        return self.ctx.enter_context(self.nc.sbuf_tensor(name, shape, dtype))

    def bank(self, name):
        return self.ctx.enter_context(self.nc.psum_tensor(name, [P, CH], F32))

    def sem(self, name):
        return self.ctx.enter_context(self.nc.semaphore(name))


def phase_norm(nc, x, wdq, wdkv, wuv, router, ln_scale, ln_bias, identity, iota, earlier, iota_tiles,
               v_scratch, xn_scratch, acc_scratch, slot_rows, cT, slots, weights, tile_expert):
    chunks = TOKENS // CH
    with ExitStack() as ctx:
        m = Memory(nc, ctx)
        x_in = [m.sb(f"x_in{u}", [P, CT, D]) for u in range(2)]
        xn = [m.sb(f"xn{u}", [P, CT, D]) for u in range(2)]
        xn2 = [m.sb(f"xn2_{u}", [P, CT, D]) for u in range(2)]
        stats = m.sb("stats", [P, 2, CT, 6])
        moments = m.sb("moments", [P, 2, CT, 2])
        var_eps = m.sb("var_eps", [P, 2, CT])
        minus_half = m.sb("minus_half", [P, CT])
        rstd = m.sb("rstd", [P, 2, CT])
        xnT_c = [m.sb(f"xnT_c{u}", [P, KD, CH]) for u in range(2)]
        hT_c = [m.sb(f"hT_c{u}", [P, KD, CH]) for u in range(2)]
        c_c = [m.sb(f"c_c{u}", [P, 2, CH]) for u in range(2)]
        v_c = [m.sb(f"v_c{u}", [P, H, CT, DH]) for u in range(2)]
        logits = m.sb("logits", [P, TILES, E])
        wdq_sb = m.sb("wdq_sb", [P, KD, LATENT])
        wdkv_sb = m.sb("wdkv_sb", [P, KD, LATENT])
        wuv_sb = m.sb("wuv_sb", [P, H * DH])
        router_sb = m.sb("router_sb", [P, KD, E])
        res_c = [m.sb(f"res_c{u}", [P, CT, D]) for u in range(2)]
        zeros = m.sb("zeros", [P, 8 * D])
        earlier_sb = m.sb("earlier_sb", [P, P])
        all_ones = m.sb("all_ones", [P, P])
        iota_tiles_sb = m.sb("iota_tiles_sb", [1, SLOT_TILES * E])
        scale_sb = m.sb("scale_sb", [P, KD])
        bias_sb = m.sb("bias_sb", [P, KD])
        ident = m.sb("ident", [P, P])
        iota_sb = m.sb("iota_sb", [P, E])
        top = m.sb("top", [P, TILES, 8])
        top_at = m.sb("top_at", [P, TILES, 8], U32)
        top_atf = m.sb("top_atf", [P, TILES, 2])
        gap = m.sb("gap", [P, TILES])
        ratio = m.sb("ratio", [P, TILES])
        denom = m.sb("denom", [P, TILES])
        chosen = [m.sb(f"chosen{n}", [P, TILES, E]) for n in range(CHOICES)]
        both = m.sb("both", [P, TILES, E])
        totals = m.sb("totals", [P, TILES, E])
        upto = [m.sb(f"upto{n}", [P, TILES, E]) for n in range(2)]
        picked = [m.sb(f"picked{n}", [P, TILES, E]) for n in range(CHOICES)]
        slots_f = m.sb("slots_f", [P, CHOICES, TILES])
        tiles_i = m.sb("tiles_i", [P, E], mybir.dt.int32)
        tiles_f = m.sb("tiles_f", [P, E])
        ends = [m.sb(f"ends{n}", [P, E]) for n in range(2)]
        starts = m.sb("starts", [P, E])
        past = m.sb("past", [1, SLOT_TILES, E])
        expert_f = m.sb("expert_f", [1, SLOT_TILES])
        t_bank = [m.bank(f"t_bank{n}") for n in range(4)]
        c_bank = [m.bank(f"c_bank{n}") for n in range(2)]
        v_bank = [m.bank(f"v_bank{n}") for n in range(2)]

        weights_in = m.sem("weights_in")
        x_loaded = [m.sem(f"x_loaded{u}") for u in range(2)]
        norm1 = m.sem("norm1")
        norm2 = m.sem("norm2")
        small = m.sem("small")
        half_set = m.sem("half_set")
        passed = m.sem("passed")
        rstd_set = m.sem("rstd_set")
        turned = m.sem("turned")
        evac_x = m.sem("evac_x")
        evac_h = m.sem("evac_h")
        latent = m.sem("latent")
        latent_out = m.sem("latent_out")
        v_done = m.sem("v_done")
        v_out_s = m.sem("v_out_s")
        v_out_v = m.sem("v_out_v")
        routed = m.sem("routed")
        routed_out = m.sem("routed_out")
        acc_set = m.sem("acc_set")
        kept = [m.sem(f"kept{u}") for u in range(2)]
        gap_set = m.sem("gap_set")
        ratio_set = m.sem("ratio_set")
        route = m.sem("route")
        counted = m.sem("counted")
        zeros_set = m.sem("zeros_set")
        cleared = m.sem("cleared")

        block = ctx.enter_context(nc.Block())
        x_t = x.rearrange("(m j p) d -> m p j d", p=P, j=CT)
        BOTH_SET = 9
        VN = 2 * CT

        def rolled(eng, chunk):
            for u in range(2):
                chunk(0, u)
            with eng.Fori(1, chunks // 2) as i:
                for u in range(2):
                    chunk(i, u)

        @block.sync
        def _(sp):
            sp.dma_start(ident[:, :], identity).then_inc(weights_in, 16)
            sp.dma_start(wdq_sb[:, :, :], wdq.rearrange("(k p) c -> p k c", p=P)).then_inc(weights_in, 16)
            sp.dma_start(wdkv_sb[:, :, :], wdkv.rearrange("(k p) c -> p k c", p=P)).then_inc(weights_in, 16)
            sp.dma_start(wuv_sb[:, :], wuv).then_inc(weights_in, 16)
            sp.dma_start(router_sb[:, :, :], router.rearrange("(k p) e -> p k e", p=P)).then_inc(weights_in, 16)
            sp.dma_start(scale_sb[:, :], ln_scale).then_inc(weights_in, 16)
            sp.dma_start(bias_sb[:, :], ln_bias).then_inc(weights_in, 16)
            sp.dma_start(iota_sb[:, :], iota).then_inc(weights_in, 16)
            sp.dma_start(earlier_sb[:, :], earlier).then_inc(weights_in, 16)
            sp.dma_start(iota_tiles_sb[:, :], iota_tiles).then_inc(weights_in, 16)

            def chunk(i, u):
                n = 2 * i + u
                need(sp, acc_set, n - 1)
                sp.dma_start(x_in[u][:, :, :], x_t[n]).then_inc(x_loaded[u], 16)

            def store(i, u):
                n = 2 * i + u
                need(sp, norm1, CT * (n + 1))
                sp.dma_start(xn_scratch[n].rearrange("(j p) d -> p j d", p=P), xn[u][:, :, :]).then_inc(kept[u], 16)
                need(sp, acc_set, n + 1)
                sp.dma_start(acc_scratch[:, bass.ds(CT * n, CT), :], res_c[u][:, :, :]).then_inc(kept[u], 16)
                need(sp, latent_out, 2 * (n + 1))
                sp.dma_start(cT[:, :, bass.ds(CH * n, CH)], c_c[u][:, :, :]).then_inc(kept[u], 16)
                need(sp, v_out_s, CT * (n + 1))
                need(sp, v_out_v, CT * (n + 1))
                sp.dma_start(v_scratch[n], v_c[u][:, :, :, :]).then_inc(kept[u], 16)

            chunk(0, 0)
            chunk(0, 1)
            with sp.Fori(0, chunks // 2 - 1) as i:
                for u in range(2):
                    chunk(i + 1, u)
                    store(i, u)
            for u in range(2):
                store(chunks // 2 - 1, u)
            for u in range(2):
                sp.wait_ge(kept[u], 64 * (chunks // 2))

        @block.vector
        def _(dve):
            STEPS = 2 * (2 * CT + 1)
            dve.wait_ge(weights_in, 16 * 10)

            def norm(i, u, which, src, dst, done):
                n = 2 * i + u
                base = STEPS * n + which * (2 * CT + 1)
                for j in range(CT):
                    nc.vector.bn_stats(stats[:, which, j, :], src[:, j, :]).then_inc(small, 1)
                dve.wait_ge(small, base + CT)
                dve.sem_inc(passed, 1)
                for j in range(CT):
                    nc.vector.bn_aggr(moments[:, which, j, :], stats[:, which, j, :]).then_inc(small, 1)
                dve.wait_ge(small, base + 2 * CT)
                nc.vector.tensor_scalar(var_eps[:, which, :], moments[:, which, :, 1], EPS, None,
                                        ALU.add).then_inc(small, 1)
                dve.wait_ge(rstd_set, 2 * n + which + 1)
                for j in range(CT):
                    nc.vector.tensor_scalar(dst[:, j, :], src[:, j, :], moments[:, which, j, 0:1],
                                            rstd[:, which, j:j + 1], ALU.subtract, ALU.mult).then_inc(done, 1)

            def chunk(i, u):
                n = 2 * i + u
                dve.wait_ge(x_loaded[u], 16 * (i + 1))
                need(dve, turned, 4 * (n - 1))
                need(dve, acc_set, n - 1)
                need(dve, kept[u], 64 * i)
                norm(i, u, 0, x_in[u], xn[u], norm1)
                dve.wait_ge(norm1, CT * (n + 1))
                norm(i, u, 1, xn[u], xn2[u], norm2)
                need(dve, latent, 2 * (n - 1))
                for k in range(KD):
                    dve.wait_ge(turned, 4 * n + 3 + k)
                    nc.vector.tensor_scalar(hT_c[u][:, k, :], t_bank[2 + k][:, :], scale_sb[:, k:k + 1],
                                            bias_sb[:, k:k + 1], ALU.mult, ALU.add).then_inc(evac_h, 1)
                need(dve, kept[u], 64 * i)
                for j in range(CT):
                    dve.wait_ge(v_done, VN * n + 2 * j + 2)
                    nc.vector.tensor_copy(v_c[u][:, H // 2:, j, :], v_bank[1][:, :].rearrange("p (h d) -> p h d", d=DH)).then_inc(v_out_v, 1)
                dve.wait_ge(routed, n + 1)
                nc.vector.tensor_copy(logits[:, bass.ds(CT * n, CT), :],
                                      c_bank[0][:, 0:CT * E].rearrange("p (j e) -> p j e", e=E)).then_inc(routed_out, 1)

            rolled(dve, chunk)

            step = [0]

            def link(ins):
                step[0] += 1
                ins.then_inc(route, 1)
                dve.wait_ge(route, step[0])

            dve.wait_ge(routed_out, chunks)
            for t in range(TILES):
                ins = nc.vector.max(top[:, t, :], logits[:, t, :])
                link(ins) if t == TILES - 1 else None
            for t in range(TILES):
                ins = nc.vector.max_index(top_at[:, t, :], top[:, t, :], logits[:, t, :])
            link(ins)
            nc.vector.tensor_tensor(gap[:, :], top[:, :, 1], top[:, :, 0], ALU.subtract).then_inc(gap_set, 1)
            link(nc.vector.tensor_copy(top_atf[:, :, :], top_at[:, :, 0:CHOICES]))
            dve.wait_ge(ratio_set, 1)
            link(nc.vector.tensor_scalar(denom[:, :], ratio[:, :], 1.0, None, ALU.add))
            link(nc.vector.reciprocal(weights[:, 0, :], denom[:, :]))
            link(nc.vector.tensor_tensor(weights[:, 1, :], weights[:, 0, :], ratio[:, :], ALU.mult))

            full = [P, TILES, E]
            for n in range(CHOICES):
                link(nc.vector.tensor_tensor(chosen[n][:, :, :], iota_sb[:, :].unsqueeze(1).broadcast_to(full),
                                             top_atf[:, :, n:n + 1].broadcast_to(full), ALU.is_equal))
            link(nc.vector.tensor_tensor(both[:, :, :], chosen[0][:, :, :], chosen[1][:, :, :], ALU.add))
            both_set = step[0]
            assert both_set == BOTH_SET
            dve.wait_ge(counted, 2)
            flat = "p (t e) -> p t e"
            link(nc.vector.tensor_copy(totals[:, :, :], t_bank[1][:, :].rearrange(flat, e=E)))
            source, at, by = totals, 0, 1
            while by < TILES:
                link(nc.vector.tensor_copy(upto[at][:, 0:by, :], source[:, 0:by, :]))
                link(nc.vector.tensor_tensor(upto[at][:, by:, :], source[:, by:, :], source[:, 0:TILES - by, :], ALU.add))
                source, at, by = upto[at], 1 - at, 2 * by
            count = source[:, TILES - 1, :]
            link(nc.vector.tensor_scalar(tiles_f[:, :], count, float(P - 1), None, ALU.add))
            link(nc.vector.tensor_copy(tiles_i[:, :], tiles_f[:, :]))
            link(nc.vector.tensor_scalar(tiles_i[:, :], tiles_i[:, :], 7, None, ALU.logical_shift_right))
            link(nc.vector.tensor_copy(tiles_f[:, :], tiles_i[:, :]))
            end, to, by = tiles_f, 0, 1
            while by < E:
                link(nc.vector.tensor_copy(ends[to][:, 0:by], end[:, 0:by]))
                link(nc.vector.tensor_tensor(ends[to][:, by:], end[:, by:], end[:, 0:E - by], ALU.add))
                end, to, by = ends[to], 1 - to, 2 * by
            link(nc.vector.tensor_tensor(starts[:, :], end[:, :], tiles_f[:, :], ALU.subtract))
            link(nc.vector.tensor_scalar(starts[:, :], starts[:, :], float(P), None, ALU.mult))

            link(nc.vector.tensor_tensor(source[:, :, :], source[:, :, :], totals[:, :, :], ALU.subtract))
            link(nc.vector.tensor_tensor(source[:, :, :], t_bank[0][:, :].rearrange(flat, e=E), source[:, :, :], ALU.add))
            link(nc.vector.tensor_tensor(source[:, :, :], source[:, :, :], starts[:, :].unsqueeze(1).broadcast_to(full), ALU.add))
            for n in range(CHOICES):
                link(nc.vector.tensor_tensor(picked[n][:, :, :], source[:, :, :], chosen[n][:, :, :], ALU.mult))
                link(nc.vector.tensor_reduce(slots_f[:, n, :], picked[n][:, :, :], AX.X, ALU.add))
            link(nc.vector.tensor_copy(slots[:, :, :], slots_f[:, :, :]))

            tiles_by_e = [1, SLOT_TILES, E]
            link(nc.vector.tensor_tensor(past[:, :, :], iota_tiles_sb[:, :].rearrange(flat, e=E),
                                         end[0:1, :].unsqueeze(1).broadcast_to(tiles_by_e), ALU.is_ge))
            link(nc.vector.tensor_reduce(expert_f[:, :], past[:, :, :], AX.X, ALU.add))
            link(nc.vector.tensor_scalar(expert_f[:, :], expert_f[:, :], float(E - 1), None, ALU.min))
            link(nc.vector.tensor_copy(tile_expert[:, :], expert_f[:, :]))

        @block.scalar
        def _(act):
            act.wait_ge(zeros_set, 1)
            for t in range(0, SLOT_TILES, 8):
                act.dma_start(slot_rows[P * t:P * (t + 8), :].rearrange("(p t) d -> p (t d)", p=P), zeros[:, :]).then_inc(cleared, 16)

            def chunk(i, u):
                n = 2 * i + u
                need(act, kept[u], 64 * i)
                need(act, routed, n - 1)
                for k in range(KD):
                    act.wait_ge(turned, 4 * n + 1 + k)
                    nc.scalar.activation(xnT_c[u][:, k, :], t_bank[k][:, :], ACT.Copy).then_inc(evac_x, 1)
                need(act, v_done, VN * (n - 1))
                for k in range(2):
                    act.wait_ge(latent, 2 * n + 1 + k)
                    nc.scalar.activation(c_c[u][:, k, :], c_bank[k][:, :], ACT.Copy).then_inc(latent_out, 1)
                for j in range(CT):
                    act.wait_ge(v_done, VN * n + 2 * j + 1)
                    nc.scalar.activation(v_c[u][:, 0:H // 2, j, :], v_bank[0][:, :].rearrange("p (h d) -> p h d", d=DH), ACT.Copy).then_inc(v_out_s, 1)

            rolled(act, chunk)
            act.wait_ge(gap_set, 1)
            nc.scalar.activation(ratio[:, :], gap[:, :], ACT.Exp).then_inc(ratio_set, 1)
            act.wait_ge(cleared, 16 * (SLOT_TILES // 8))

        @block.gpsimd
        def _(pool):
            def chunk(i, u):
                n = 2 * i + u
                for which in range(2):
                    pool.wait_ge(small, (4 * CT + 2) * n + (which + 1) * (2 * CT + 1))
                    nc.gpsimd.tensor_tensor(rstd[:, which, :], var_eps[:, which, :], minus_half[:, :], ALU.pow
                                            ).then_inc(rstd_set, 1)
                pool.wait_ge(norm1, CT * (n + 1))
                need(pool, kept[u], 64 * i)
                nc.gpsimd.tensor_tensor(res_c[u][:, :, :], x_in[u][:, :, :], xn[u][:, :, :],
                                        ALU.add).then_inc(acc_set, 1)

            nc.gpsimd.memset(zeros[:, :], 0.0).then_inc(zeros_set, 1)
            nc.gpsimd.memset(all_ones[:, :], 1.0).then_inc(half_set, 1)
            nc.gpsimd.memset(minus_half[:, :], -0.5).then_inc(half_set, 1)
            pool.wait_ge(half_set, 2)
            rolled(pool, chunk)

        @block.tensor
        def _(pe):
            pe.wait_ge(weights_in, 16 * 10)

            def chunk(i, u):
                n = 2 * i + u
                for which, (src, done, evac) in enumerate(((xn[u], norm1, evac_x), (xn2[u], norm2, evac_h))):
                    pe.wait_ge(done, CT * (n + 1))
                    for k in range(KD):
                        need(pe, evac, KD * (n - 1) + k + 1)
                        for j in range(CT):
                            mm = nc.tensor.transpose(t_bank[2 * which + k][:, j * P:(j + 1) * P],
                                                     src[:, j, k * P:(k + 1) * P], ident[:, :])
                        mm.then_inc(turned, 1)
                need(pe, routed_out, n)
                need(pe, latent_out, 2 * n)
                pe.wait_ge(evac_h, KD * (n + 1))
                for c, w in enumerate((wdq_sb, wdkv_sb)):
                    for k in range(KD):
                        mm = nc.tensor.matmul(c_bank[c][:, :], w[:, k, :], hT_c[u][:, k, :], start=(k == 0), stop=(k == KD - 1))
                    mm.then_inc(latent, 1)
                pe.wait_ge(latent_out, 2 * (n + 1))
                for j in range(CT):
                    for half, out_sem in enumerate((v_out_s, v_out_v)):
                        need(pe, out_sem, CT * n + j)
                        nc.tensor.matmul(v_bank[half][:, :], c_c[u][:, 1, j * P:(j + 1) * P],
                                         wuv_sb[:, half * CH:(half + 1) * CH], start=True, stop=True).then_inc(v_done, 1)
                pe.wait_ge(evac_x, KD * (n + 1))
                for j in range(CT):
                    for k in range(KD):
                        mm = nc.tensor.matmul(c_bank[0][:, j * E:(j + 1) * E], xnT_c[u][:, k, j * P:(j + 1) * P],
                                              router_sb[:, k, :], start=(k == 0), stop=(k == KD - 1))
                mm.then_inc(routed, 1)

            rolled(pe, chunk)
            pe.wait_ge(half_set, 2)
            pe.wait_ge(route, BOTH_SET)
            for n, w in enumerate((earlier_sb, all_ones)):
                nc.tensor.matmul(t_bank[n][:, :], w[:, :], both[:, :, :].rearrange("p t e -> p (t e)"), start=True, stop=True
                                 ).then_inc(counted, 1)


def phase_experts(nc, w_gu, w_dn, w_qk, cos_t, sin_t, identity, xn_scratch, slot_rows, y_rows, qk_scratch,
                  cT, slots, tile_expert):
    PER = 16
    STEPS = PAIRS * 8
    FIRST = STEPS - SLOT_TILES
    assert FIRST % PER == 0 and SLOT_TILES % PER == 0
    with ExitStack() as ctx:
        m = Memory(nc, ctx)
        gu_sb = m.sb("gu_sb", [P, E, KD, 2 * F])
        dn_sb = m.sb("dn_sb", [P, E, F // P, D])
        qk_sb = [m.sb(f"qk_sb{u}", [P, 4, P]) for u in range(2)]
        ident = m.sb("ident2", [P, P])
        cos_sb = m.sb("cos_sb", [P, S])
        sin_sb = m.sb("sin_sb", [P, S])
        by_cos = [m.sb(f"by_cos{u}", [P, CH]) for u in range(2)]
        by_sin = [m.sb(f"by_sin{u}", [P, CH]) for u in range(2)]
        rot = [m.sb(f"rot{u}", [P, CH]) for u in range(2)]
        hi = [m.sb(f"hi{u}", [P, CH], F32R) for u in range(2)]
        lo = [m.sb(f"lo{u}", [P, CH], F32R) for u in range(2)]
        STAGES = 4
        stage = [m.sb(f"stage{n}", [P, D]) for n in range(STAGES)]
        rows = [m.sb(f"rows{u}", [P, D]) for u in range(2)]
        rowsT = [m.sb(f"rowsT{u}", [P, KD, P]) for u in range(2)]
        silu = [m.sb(f"silu{u}", [P, F]) for u in range(2)]
        gated = [m.sb(f"gated{u}", [P, F]) for u in range(2)]
        gatedT = [m.sb(f"gatedT{u}", [P, F // P, P]) for u in range(2)]
        y = [m.sb(f"y{u}", [P, D]) for u in range(2)]
        pr_bank = [m.bank(f"pr_bank{n}") for n in range(2)]
        xt_bank = m.bank("xt_bank")
        gu_bank = [m.bank(f"gu_bank{n}") for n in range(2)]
        gt_bank = m.bank("gt_bank")
        y_bank = m.bank("y_bank")

        tables_in = m.sem("tables_in")
        experts_in = m.sem("experts_in")
        passed2 = m.sem("passed2")
        w_in = [m.sem(f"w_in{u}") for u in range(2)]
        pr_done = m.sem("pr_done")
        mul_done = m.sem("mul_done")
        rot_done = m.sem("rot_done")
        hi_done = m.sem("hi_done")
        lo_done = m.sem("lo_done")
        stored = [m.sem(f"stored{u}") for u in range(2)]
        staged = [m.sem(f"staged{n}") for n in range(STAGES)]
        scattered = [m.sem(f"scattered{n}") for n in range(STAGES)]
        rows_in = [m.sem(f"rows_in{u}") for u in range(2)]
        xt_done = m.sem("xt_done")
        xt_set = m.sem("xt_set")
        g_done = m.sem("g_done")
        silu_done = m.sem("silu_done")
        gated_set = m.sem("gated_set")
        gt_done = m.sem("gt_done")
        gt_set = m.sem("gt_set")
        y_done = m.sem("y_done")
        y_set = m.sem("y_set")
        y_kept = [m.sem(f"y_kept{u}") for u in range(2)]

        block = ctx.enter_context(nc.Block())

        def rolled(eng, step):
            def turn(i, tiles):
                for j in range(PER):
                    step(PER * i + j, i, j, tiles)
            turn(0, False)
            with eng.Fori(1, FIRST // PER) as i:
                turn(i, False)
            turn(FIRST // PER, True)
            with eng.Fori(FIRST // PER + 1, STEPS // PER - 1) as i:
                turn(i, True)
            turn(STEPS // PER - 1, True)
            for j in range(3):
                step(STEPS + j, STEPS // PER, j, True)

        def uses(i, j):
            return PER // 2 * i + j // 2 - FIRST // 2

        @block.sync
        def _(sp):
            def load_pair(pair, u):
                sp.dma_start(qk_sb[u][:, :, :], w_qk[pair % (H // 2)]).then_inc(w_in[u], 16)

            def load_rows(f, i, j):
                need(sp, xt_done, f - 1)
                sp.dma_start(rows[j % 2][:, :], slot_rows.rearrange("(t p) d -> t p d", p=P)[f]).then_inc(rows_in[j % 2], 16)

            load_pair(0, 0)
            sp.dma_start(cos_sb[:, :], cos_t).then_inc(tables_in, 16)
            sp.dma_start(sin_sb[:, :], sin_t).then_inc(tables_in, 16)
            sp.dma_start(ident[:, :], identity).then_inc(tables_in, 16)

            def step(s, i, j, tiles):
                u = j // 8 % 2
                f = s - FIRST
                if tiles and isinstance(f, int) and f == 0:
                    for n in range(STAGES):
                        sp.wait_ge(scattered[n], 32 * TILES // STAGES)
                    load_rows(0, i, j)
                    load_rows(1, i, j + 1)
                if within(s, STEPS):
                    if j % 8 == 2 and (not isinstance(i, int) or 2 * i + u + 1 < PAIRS):
                        need(sp, pr_done, 16 * (2 * i + u))
                        sp.sem_inc(passed2, 1)
                        load_pair(2 * i + u + 1, 1 - u)
                    at = slice(CH * (j % 4), CH * (j % 4 + 1))
                    sp.wait_ge(hi_done, s + 1)
                    sp.dma_start(qk_scratch[2 * i + u][:, 2 * (j % 8 // 4), at], hi[j % 2][:, :].bitcast(F32)).then_inc(stored[j % 2], 16)
                    sp.wait_ge(lo_done, s + 1)
                    sp.dma_start(qk_scratch[2 * i + u][:, 2 * (j % 8 // 4) + 1, at], lo[j % 2][:, :].bitcast(F32)).then_inc(stored[j % 2], 16)
                if tiles and within(f, SLOT_TILES) and within(f + 2, SLOT_TILES):
                    load_rows(f + 2, i, j)
                if tiles and within(f - 3, SLOT_TILES):
                    sp.wait_ge(y_set, f - 2)
                    sp.dma_start(y_rows.rearrange("(t p) d -> t p d", p=P)[f - 3], y[(j - 3) % 2][:, :]).then_inc(y_kept[(j - 3) % 2], 16)

            rolled(sp, step)
            for u in range(2):
                sp.wait_ge(stored[u], 32 * (STEPS // 2))
                sp.wait_ge(y_kept[u], 16 * (SLOT_TILES // 2))

        @block.tensor
        def _(pe):
            def step(s, i, j, tiles):
                u = j // 8 % 2
                f = s - FIRST
                if within(s, STEPS):
                    if j % 8 == 0:
                        pe.wait_ge(w_in[u], 16 * (i + 1))
                    sequence = (2 * i + u) // (H // 2)
                    for n in range(2):
                        need(pe, mul_done, 2 * (s - 1) + n + 1)
                        nc.tensor.matmul(pr_bank[n][:, :], qk_sb[u][:, 2 * (j % 8 // 4) + n, :],
                                         cT[:, j % 8 // 4, bass.ds(S * sequence + CH * (j % 4), CH)],
                                         start=True, stop=True).then_inc(pr_done, 1)
                if not tiles:
                    return
                if within(f, SLOT_TILES):
                    pe.wait_ge(tables_in, 48)
                    pe.wait_ge(rows_in[j % 2], 16 * (uses(i, j) + 1))
                    need(pe, xt_set, f)
                    for k in range(KD):
                        mm = nc.tensor.transpose(xt_bank[:, P * k:P * (k + 1)], rows[j % 2][:, P * k:P * (k + 1)], ident[:, :])
                    mm.then_inc(xt_done, 1)
                if within(f - 2, SLOT_TILES):
                    pe.wait_ge(gated_set, f - 1)
                    need(pe, gt_set, f - 2)
                    for k in range(F // P):
                        mm = nc.tensor.transpose(gt_bank[:, P * k:P * (k + 1)], gated[j % 2][:, P * k:P * (k + 1)], ident[:, :])
                    mm.then_inc(gt_done, 1)
                if within(f - 1, SLOT_TILES):
                    expert = pe.value_load(tile_expert[0:1, bass.ds(f - 1, 1)], min_val=0, max_val=E - 1)
                    pe.wait_ge(experts_in, 32)
                    pe.wait_ge(xt_set, f)
                    need(pe, gated_set, f - 2)
                    for k in range(KD):
                        mm = nc.tensor.matmul(gu_bank[(j - 1) % 2][:, :], rowsT[(j - 1) % 2][:, k, :],
                                              gu_sb[:, bass.ds(expert, 1), k, :].rearrange("p e f -> p (e f)"),
                                              start=(k == 0), stop=(k == KD - 1))
                    mm.then_inc(g_done, 1)
                if within(f - 3, SLOT_TILES):
                    expert = pe.value_load(tile_expert[0:1, bass.ds(f - 3, 1)], min_val=0, max_val=E - 1)
                    pe.wait_ge(gt_set, f - 2)
                    need(pe, y_set, f - 3)
                    for k in range(F // P):
                        mm = nc.tensor.matmul(y_bank[:, 0:D], gatedT[(j - 3) % 2][:, k, :],
                                              dn_sb[:, bass.ds(expert, 1), k, :].rearrange("p e d -> p (e d)"),
                                              start=(k == 0), stop=(k == F // P - 1))
                    mm.then_inc(y_done, 1)

            rolled(pe, step)

        @block.scalar
        def _(act):
            act.dma_start(gu_sb[:, :, :, :], w_gu).then_inc(experts_in, 16)
            act.dma_start(dn_sb[:, :, :, :], w_dn).then_inc(experts_in, 16)

            def step(s, i, j, tiles):
                f = s - FIRST
                if within(s - 1, STEPS):
                    v = (j - 1) % 2
                    act.wait_ge(rot_done, s)
                    need(act, lo_done, s - 2)
                    need(act, stored[v], 32 * (8 * i + (j - 1) // 2))
                    nc.scalar.activation(hi[v][:, :], rot[v][:, :], ACT.Copy).then_inc(hi_done, 1)
                if tiles and within(f - 2, SLOT_TILES):
                    act.wait_ge(gt_done, f - 1)
                    need(act, y_done, f - 3)
                    nc.scalar.activation(gatedT[j % 2][:, :, :], gt_bank[:, 0:F].rearrange("p (k t) -> p k t", t=P), ACT.Copy).then_inc(gt_set, 1)
                if tiles and within(f - 1, SLOT_TILES):
                    act.wait_ge(g_done, f)
                    need(act, gated_set, f - 2)
                    nc.scalar.activation(silu[(j - 1) % 2][:, :], gu_bank[(j - 1) % 2][:, 0:F], ACT.Silu).then_inc(silu_done, 1)

            rolled(act, step)

        @block.vector
        def _(dve):
            dve.wait_ge(tables_in, 48)

            def step(s, i, j, tiles):
                f = s - FIRST
                if within(s, STEPS):
                    need(dve, rot_done, s - 1)
                    at = slice(CH * (j % 4), CH * (j % 4 + 1))
                    for n, (out, table) in enumerate(((by_cos[j % 2], cos_sb), (by_sin[j % 2], sin_sb))):
                        dve.wait_ge(pr_done, 2 * s + n + 1)
                        nc.vector.tensor_tensor(out[:, :], pr_bank[n][:, :], table[:, at], ALU.mult).then_inc(mul_done, 1)
                if within(s - 1, STEPS):
                    v = (j - 1) % 2
                    dve.wait_ge(hi_done, s)
                    need(dve, stored[v], 32 * (8 * i + (j - 1) // 2))
                    nc.vector.tensor_tensor(lo[v][:, :], rot[v][:, :], hi[v][:, :], ALU.subtract).then_inc(lo_done, 1)
                if tiles and within(f, SLOT_TILES):
                    dve.wait_ge(xt_done, f + 1)
                    need(dve, g_done, f - 1)
                    nc.vector.tensor_copy(rowsT[j % 2][:, :, :], xt_bank[:, 0:D].rearrange("p (k t) -> p k t", t=P)).then_inc(xt_set, 1)
                if within(s, STEPS):
                    dve.wait_ge(mul_done, 2 * (s + 1))
                    need(dve, lo_done, s - 1)
                    need(dve, hi_done, s - 1)
                    nc.vector.tensor_tensor(rot[j % 2][:, :], by_cos[j % 2][:, :], by_sin[j % 2][:, :], ALU.add).then_inc(rot_done, 1)
                if tiles and within(f - 1, SLOT_TILES):
                    dve.wait_ge(silu_done, f)
                    need(dve, gt_done, f - 2)
                    nc.vector.tensor_tensor(gated[(j - 1) % 2][:, :], silu[(j - 1) % 2][:, :], gu_bank[(j - 1) % 2][:, F:2 * F], ALU.mult
                                            ).then_inc(gated_set, 1)
                if tiles and within(f - 3, SLOT_TILES):
                    dve.wait_ge(y_done, f - 2)
                    need(dve, y_kept[(j - 3) % 2], 16 * uses(i, j - 3))
                    nc.vector.tensor_copy(y[(j - 3) % 2][:, :], y_bank[:, 0:D]).then_inc(y_set, 1)

            rolled(dve, step)

        @block.gpsimd
        def _(pool):
            def stage_in(t):
                if t >= STAGES:
                    pool.wait_ge(scattered[t % STAGES], 32 * (t // STAGES))
                pool.dma_start(stage[t % STAGES][:, :], xn_scratch.rearrange("n (j p) d -> (n j) p d", p=P)[t]).then_inc(staged[t % STAGES], 16)

            for t in range(STAGES - 1):
                stage_in(t)
            for t in range(TILES):
                if t + STAGES - 1 < TILES:
                    stage_in(t + STAGES - 1)
                pool.wait_ge(staged[t % STAGES], 16 * (t // STAGES + 1))
                for n in range(CHOICES):
                    nc.gpsimd.indirect_dma_start(slot_rows, bass.IndirectOffsetOnAxis(ap=slots[:, n, t:t + 1], axis=0),
                                                 stage[t % STAGES][:, :], None).then_inc(scattered[t % STAGES], 16)


def phase_attention(nc, identity, w_out, qk_scratch, v_scratch, acc_scratch, y_rows, slots, weights, out):
    CHUNKS = PAIRS * 8
    GROUPS = CHUNKS // 2
    PER = 16
    ST = 16
    Q_LOAD, K_LOAD = 6 * 16, 14 * 16
    ADDS = (5, 6)
    AFTER = ({0: 1, 1: 1, 3: 2, 4: 3, 5: 4, 7: 5}, {0: 1, 1: 2, 3: 3, 4: 4, 5: 5, 7: 6})
    with ExitStack() as ctx:
        m = Memory(nc, ctx)
        q_hh = [m.sb(f"q_hh{u}", [P, S], F32R) for u in range(2)]
        q_lm = [m.sb(f"q_lm{u}", [DH + 1, S], F32R) for u in range(2)]
        k_hl = [[m.sb(f"k_hl{w}{u}", [P, S], F32R) for u in range(2)] for w in range(2)]
        k_h1 = [[m.sb(f"k_h1{w}{u}", [DH + 1, S], F32R) for u in range(2)] for w in range(2)]
        v_sb = [[m.sb(f"v_sb{w}{u}", [P, KT, DH]) for u in range(2)] for w in range(2)]
        acc = m.sb("acc", [P, TILES, D])
        slot_now = [m.sb(f"slot_now{n}", [P, 1], U32) for n in range(CHOICES)]
        y_in = [m.sb(f"y_in{n}", [P, D]) for n in range(CHOICES)]
        w_out_sb = m.sb("w_out_sb", [P, H // 2, D])
        probs = m.sb("probs", [P, 8, CH])
        pair_sum = [m.sb(f"pair_sum{n}", [P, 2, CH]) for n in range(2)]
        sums = [m.sb(f"sums{n}", [P, 2, CH]) for n in range(2)]
        rsum = m.sb("rsum", [P, CH])
        normed = [m.sb(f"normed{n}", [P, CH]) for n in range(2)]
        maxes = [m.sb(f"maxes{n}", [P, CT, 4]) for n in range(2)]
        neg_max = [m.sb(f"neg_max{n}", [P, CT, DH + 1]) for n in range(2)]
        ident = m.sb("ident3", [P, P])
        ones_sb = m.sb("ones_sb", [P, DH])
        s_bank = [m.bank(f"s_bank{n}") for n in range(2)]
        a_bank = [m.bank(f"a_bank{n}") for n in range(2)]
        o_bank = [m.bank(f"o_bank{n}") for n in range(2)]
        m_bank = [m.bank(f"m_bank{n}") for n in range(2)]

        consts_in = m.sem("consts_in")
        consts_set = m.sem("consts_set")
        q_in = [m.sem(f"q_in{n}") for n in range(QC)]
        k_in = [m.sem(f"k_in{w}") for w in range(2)]
        s_done = m.sem("s_done")
        exp_done = m.sem("exp_done")
        a_done = m.sem("a_done")
        max_done = [m.sem(f"max_done{n}") for n in range(2)]
        negmax_set = m.sem("negmax_set")
        row_done = m.sem("row_done")
        row_set = m.sem("row_set")
        pv_done = m.sem("pv_done")
        pair_done = m.sem("pair_done")
        add_done = m.sem("add_done")
        l_done = m.sem("l_done")
        rsum_set = m.sem("rsum_set")
        norm_done = m.sem("norm_done")
        op_done = m.sem("op_done")
        acc_done3 = m.sem("acc_done3")
        out_done = m.sem("out_done")
        acc_in = m.sem("acc_in")
        slot_set = m.sem("slot_set")
        fetched = [m.sem(f"fetched{n}") for n in range(CHOICES)]
        passed3, passed4 = m.sem("passed3"), m.sem("passed4")
        mixed = m.sem("mixed")

        block = ctx.enter_context(nc.Block())

        def rolled(eng, chunk):
            def turn(i, cs):
                for c in cs:
                    chunk(PER * i + c, i, c)
            turn(-1, (PER - 3, PER - 2, PER - 1))
            turn(0, range(PER))
            with eng.Fori(1, CHUNKS // PER - 1) as i:
                turn(i, range(PER))
            turn(CHUNKS // PER - 1, range(PER))
            turn(CHUNKS // PER, (0, 1))

        def group(i, c):
            return PER // 2 * i + c // 2

        def ahead(i, c, n):
            return i + (c + n) // PER, (c + n) % PER

        def adds(i, c, n):
            return PER // 2 * sum(ADDS) * i + sum(ADDS) * (c // 2) + ADDS[0] * (c % 2) + AFTER[c % 2][n]

        @block.sync
        def _(sp):
            def load_q(pair, n):
                at = slice(CH * n, CH * (n + 1))
                for u in range(2):
                    src = qk_scratch[pair][DH * u:DH * (u + 1), :, at]
                    for dst, kind in ((q_hh[u][0:DH, at], 0), (q_hh[u][DH:P, at], 0), (q_lm[u][0:DH, at], 1)):
                        sp.dma_start(dst.bitcast(F32), src[:, kind, :]).then_inc(q_in[n], 16)

            def load_k(pair, w):
                b, pair_of_b = pair // (H // 2), pair % (H // 2)
                for u in range(2):
                    src = qk_scratch[pair][DH * u:DH * (u + 1), :, :]
                    for dst, kind in ((k_hl[w][u][0:DH, :], 2), (k_hl[w][u][DH:P, :], 3), (k_h1[w][u][0:DH, :], 2)):
                        sp.dma_start(dst.bitcast(F32), src[:, kind, :]).then_inc(k_in[w], 16)
                    for c in range(QC):
                        sp.dma_start(v_sb[w][u][:, CT * c:CT * (c + 1), :],
                                     v_scratch[QC * b + c][:, bass.ds(2 * pair_of_b + u, 1), :, :].rearrange("p h j d -> p (h j) d")
                                     ).then_inc(k_in[w], 16)

            load_k(0, 0)
            for n in range(QC):
                load_q(0, n)
            sp.dma_start(ident[:, :], identity).then_inc(consts_in, 16)
            sp.dma_start(w_out_sb[:, :, :], w_out.rearrange("(h p) n -> p h n", p=P)).then_inc(consts_in, 16)
            sp.dma_start(acc[:, :, :], acc_scratch).then_inc(acc_in, 16)
            load_k(1, 1)

            def turn(i, last):
                for w in range(2):
                    if last and w == 1:
                        return
                    for n in range(QC):
                        sp.wait_ge(s_done, 16 * (PER * i + 8 * w + 2 * n + 2))
                        sp.sem_inc(passed4, 1)
                        load_q(2 * i + w + 1, n)
                    if not last:
                        sp.wait_ge(pv_done, 4 * (PER * i + 8 * w + 8))
                        sp.sem_inc(passed4, 1)
                        load_k(2 * i + w + 2, w)

            with sp.Fori(0, PAIRS // 2 - 1) as i:
                turn(i, False)
            turn(PAIRS // 2 - 1, True)
            sp.wait_ge(acc_done3, 2 * GROUPS)
            sp.wait_ge(mixed, CHUNKS // 2)
            sp.dma_start(out.rearrange("(t p) d -> p t d", p=P), acc[:, :, :]).then_inc(out_done, 16)
            sp.wait_ge(out_done, 16)

        @block.tensor
        def _(pe):
            pe.wait_ge(consts_in, 32)
            pe.wait_ge(consts_set, 9)

            def scores_T(k, i, c, n):
                w, u, q = c // 8, n % 2, CH * (c // 2 % QC)
                tile = 8 * (c % 2) + n // 2
                keys = slice(P * tile, P * (tile + 1))
                if n == 0 and c % 2 == 0:
                    pe.wait_ge(row_set, k + 2)
                need(pe, exp_done, 16 * k + n - 1)
                nc.tensor.matmul(s_bank[n % 2][:, :], k_hl[w][u][:, keys], q_hh[u][:, q:q + CH], start=True, stop=False)
                nc.tensor.matmul(s_bank[n % 2][:, :], k_h1[w][u][:, keys], q_lm[u][:, q:q + CH], start=False, stop=True
                                 ).then_inc(s_done, 1)

            def scores(k, i, c, n):
                i, c = ahead(i, c, 3)
                w, u, slot = c // 8, c % 2, c // 2 % QC
                q = CH * slot + P * (n // 4)
                if n == 0 and c % 8 == 0:
                    pe.wait_ge(k_in[w], K_LOAD * (i + 1))
                if n == 0 and c % 2 == 0:
                    pe.wait_ge(q_in[slot], Q_LOAD * (2 * i + w + 1))
                need(pe, max_done[n % 2], 8 * (k + 3) + n // 2)
                nc.tensor.matmul(a_bank[n % 2][:, :], q_hh[u][:, q:q + P], k_hl[w][u][:, CH * (n % 4):CH * (n % 4 + 1)],
                                 start=True, stop=True).then_inc(a_done, 1)

            def values(k, i, c, r):
                if r == 0 and c % 2 == 0:
                    need(pe, norm_done, group(i, c) - 1)
                for n in range(4 * r, 4 * r + 4):
                    u = n % 2
                    if u == 0:
                        pe.wait_ge(exp_done, 16 * k + n + 2)
                    mm = nc.tensor.matmul(o_bank[c // 2 % 2][DH * u:DH * (u + 1), :], v_sb[c // 8][u][:, 8 * (c % 2) + n // 2, :],
                                          probs[:, n % 8, :], start=(c % 2 == 0 and n < 2), stop=(c % 2 == 1 and n >= ST - 2))
                mm.then_inc(pv_done, 1)

            def output(k, i, c):
                i, c = ahead(i, c, -3)
                pair = (2 * i + c // 8) % (H // 2)
                pe.wait_ge(norm_done, group(i, c) + 1)
                need(pe, row_set, min(k + 2, CHUNKS) if isinstance(k, int) else k + 2)
                for half in range(2):
                    for t in range(2):
                        tile = slice(P * (2 * half + t), P * (2 * half + t + 1))
                        mm = nc.tensor.matmul(m_bank[half][:, D * t:D * (t + 1)], normed[c // 2 % 2][:, tile],
                                              w_out_sb[:, bass.ds(pair, 1), :].rearrange("p h n -> p (h n)"), start=True, stop=True)
                    mm.then_inc(op_done, 1)

            def chunk(k, i, c):
                g = group(i, c)
                for r in range(4):
                    for t in range(4):
                        if within(k, CHUNKS):
                            scores_T(k, i, c, 4 * r + t)
                        if within(k + 3, CHUNKS):
                            scores(k, i, c, 4 * r + t)
                    if r == 0 and within(k - 1, CHUNKS):
                        values(k - 1, *ahead(i, c, -1), 3)
                    if r > 0 and within(k, CHUNKS):
                        values(k, i, c, r - 1)
                    if r == 0 and c % 2 == 1 and within(g - 1, GROUPS):
                        output(k, i, c)
                    if r == 2 and within(k + 2, CHUNKS):
                        pe.wait_ge(negmax_set, k + 3)
                        need(pe, row_set, k + 2)
                        need(pe, acc_done3, 2 * (g - 2 + c % 2) + 1)
                        for t in range(CT):
                            mm = nc.tensor.transpose(m_bank[0][0:DH + 1, P * t:P * (t + 1)], neg_max[c % 2][:, t, :], ident[:, :])
                        mm.then_inc(row_done, 1)
                    if r == 1 and c % 2 == 0 and within(g - 1, GROUPS):
                        pe.wait_ge(add_done, sum(ADDS) * g)
                        need(pe, acc_done3, 2 * (g - 1))
                        for u in range(2):
                            mm = nc.tensor.matmul(m_bank[1][DH * u:DH * (u + 1), :], ones_sb[:, :], sums[(c // 2 - 1) % 2][:, u, :],
                                                  start=True, stop=True)
                        mm.then_inc(l_done, 1)

            rolled(pe, chunk)

        @block.scalar
        def _(act):
            def chunk(k, i, c):
                for n in range(ST):
                    if within(k, CHUNKS):
                        if n % 4 == 0:
                            need(act, pv_done, 4 * k + n // 4 - 1)
                        if n % 2 == 0 and (n >= 8 or not isinstance(k, int) or k > 0):
                            before, pair = (k, n // 2 - 4) if n >= 8 else (k - 1, n // 2 + 4)
                            if pair % 4 >= 2:
                                act.wait_ge(pair_done, 2 * before + pair // 4 + 1)
                            else:
                                act.wait_ge(add_done, adds(*(ahead(i, c, 0) if n >= 8 else ahead(i, c, -1)), pair))
                        act.wait_ge(s_done, 16 * k + n + 1)
                        nc.scalar.activation(probs[:, n % 8, :], s_bank[n % 2][:, :], ACT.Exp, scale=SCALE).then_inc(exp_done, 1)
                    if n == 11 and within(k + 2, CHUNKS):
                        q = CH * (ahead(i, c, 2)[1] // 2 % QC)
                        act.wait_ge(row_done, k + 3)
                        nc.scalar.activation(q_lm[c % 2][DH:DH + 1, q:q + CH], m_bank[0][DH:DH + 1, :], ACT.Copy).then_inc(row_set, 1)

            rolled(act, chunk)

        @block.vector
        def _(dve):
            for n in range(2):
                nc.vector.memset(neg_max[n][:, :, :], 0.0).then_inc(consts_set, 1)
                nc.vector.memset(q_lm[n][DH:DH + 1, :].bitcast(F32), 0.0).then_inc(consts_set, 1)
                for w in range(2):
                    nc.vector.memset(k_h1[w][n][DH:DH + 1, :].bitcast(F32), 1.0).then_inc(consts_set, 1)
            nc.vector.memset(ones_sb[:, :], 1.0).then_inc(consts_set, 1)
            dve.wait_ge(consts_set, 9)
            dve.wait_ge(acc_in, 16)

            def add_output(k, i, c, half):
                g = group(i, c) - 1
                i1, c1 = ahead(i, c, -3)
                tile = TILES // B * (i1 // (PAIRS // B // 2)) + CT * (c1 // 2 % QC) + 2 * half
                at = acc[:, bass.ds(tile, 2), :]
                dve.wait_ge(op_done, 2 * g + half + 1)
                need(dve, acc_done3, 2 * g + half - 7)
                need(dve, mixed, g + 1)
                nc.vector.tensor_tensor(at, m_bank[half][:, :].rearrange("p (t n) -> p t n", n=D), at, ALU.add
                                        ).then_inc(acc_done3, 1)

            def add_pair(k, i, c, n):
                dve.wait_ge(exp_done, 16 * k + 8 * n + 8)
                if not isinstance(k, int) or k > 0:
                    dve.wait_ge(add_done, adds(*ahead(i, c, -1), 4 * n + 3))
                nc.vector.tensor_tensor(pair_sum[n][:, :, :], probs[:, 4:6, :], probs[:, 6:8, :], ALU.add).then_inc(pair_done, 1)

            def chunk(k, i, c):
                g = group(i, c)
                for r in range(4):
                    for n in range(4 * r, 4 * r + 4):
                        if within(k + 3, CHUNKS):
                            dve.wait_ge(a_done, 16 * (k + 3) + n + 1)
                            nc.vector.tensor_reduce(maxes[(c + 1) % 2][:, r, n % 4:n % 4 + 1], a_bank[n % 2][:, :], AX.X, ALU.max
                                                    ).then_inc(max_done[n % 2], 1)
                        if n == 1 and within(k - 1, CHUNKS):
                            add_pair(k - 1, *ahead(i, c, -1), 1)
                        if n == 9 and within(k, CHUNKS):
                            add_pair(k, i, c, 0)
                        if r == 1 and n % 2 == 1 and c % 2 == 1 and within(g - 1, GROUPS):
                            add_output(k, i, c, n % 4 // 2)
                        if r >= 2 and n % 2 == 1 and c % 2 == 0 and within(g - 1, GROUPS):
                            part = slice(P * ((n - 8) // 2), P * ((n - 8) // 2 + 1))
                            dve.wait_ge(l_done, g)
                            need(dve, norm_done, g - 1)
                            nc.vector.reciprocal(rsum[:, part], m_bank[1][:, part]).then_inc(rsum_set, 1)
                if c % 2 == 1 and within(k, CHUNKS):
                    n, tile = c // 2 % 2, 4 * i + c // 4
                    dve.wait_ge(fetched[n], 16 * (tile + 1))
                    need(dve, acc_done3, 2 * g)
                    need(dve, mixed, g)
                    at = acc[:, bass.ds(tile, 1), :].rearrange("p t d -> p (t d)")
                    nc.vector.scalar_tensor_tensor(at, y_in[n][:, :], weights[:, n, bass.ds(tile, 1)], at, ALU.mult, ALU.add
                                                   ).then_inc(mixed, 1)
                if within(k + 3, CHUNKS):
                    for n in range(2):
                        dve.wait_ge(max_done[n], 8 * (k + 4))
                    need(dve, row_done, k + 2)
                    nc.vector.tensor_reduce(neg_max[(c + 1) % 2][:, :, DH:DH + 1], maxes[(c + 1) % 2][:, :, :], AX.X, ALU.max, negate=True
                                            ).then_inc(negmax_set, 1)
                if c % 2 == 0 and within(g - 1, GROUPS):
                    dve.wait_ge(rsum_set, 4 * g)
                    dve.wait_ge(pv_done, 4 * k)
                    need(dve, op_done, 2 * (g - 2))
                    v = (c // 2 - 1) % 2
                    nc.vector.tensor_tensor(normed[v][:, :], o_bank[v][:, :], rsum[:, :], ALU.mult).then_inc(norm_done, 1)

            rolled(dve, chunk)

        @block.gpsimd
        def _(pool):
            def chunk(k, i, c):
                if not within(k, CHUNKS):
                    return
                g = group(i, c)
                if c % 2 == 0:
                    n, tile = c // 2 % 2, 4 * i + c // 4
                    need(pool, mixed, g - 1)
                    need(pool, fetched[n], 16 * tile)
                    nc.gpsimd.tensor_copy(slot_now[n][:, :], slots[:, n, bass.ds(tile, 1)]).then_inc(slot_set, 1)
                    pool.wait_ge(slot_set, g + 1)
                    pool.sem_inc(passed3, 1)
                    nc.gpsimd.indirect_dma_start(y_in[n][:, :], None, y_rows, bass.IndirectOffsetOnAxis(ap=slot_now[n][:, :], axis=0)
                                                 ).then_inc(fetched[n], 16)
                    need(pool, l_done, g - 1)
                total = sums[c // 2 % 2]
                for pair in ((1, 3, 4, 5, 7) if c % 2 == 0 else (0, 1, 3, 4, 5, 7)):
                    if pair % 4 == 3:
                        pool.wait_ge(pair_done, 2 * k + pair // 4 + 1)
                        term = pair_sum[pair // 4][:, :, :]
                    else:
                        pool.wait_ge(exp_done, 16 * k + 2 * pair + 2)
                        term = probs[:, 2 * (pair % 4):2 * (pair % 4) + 2, :]
                    first = c % 2 == 0 and pair == 1
                    need(pool, add_done, adds(i, c, pair) - 1)
                    nc.gpsimd.tensor_tensor(total[:, :, :], probs[:, 0:2, :] if first else total[:, :, :], term, ALU.add
                                            ).then_inc(add_done, 1)

            rolled(pool, chunk)


def program(nc, x, wdq, wdkv, w_qk, wuv, w_out, ln_scale, ln_bias, router, w_gu, w_dn,
            identity, iota, earlier, iota_tiles, cos_t, sin_t, out):
    def scratch(name, shape):
        return nc.dram_tensor(name, shape, F32).ap()

    v_scratch = scratch("v_scratch", (TOKENS // CH, P, H, CT, DH))
    qk_scratch = scratch("qk_scratch", (PAIRS, P, 4, S))
    xn_scratch = scratch("xn_scratch", (TOKENS // CH, CH, D))
    acc_scratch = scratch("acc_scratch", (P, TILES, D))
    slot_rows = scratch("slot_rows", (SLOT_TILES * P, D))
    y_rows = scratch("y_rows", (SLOT_TILES * P, D))
    with ExitStack() as ctx:
        slots = ctx.enter_context(nc.sbuf_tensor("slots", [P, CHOICES, TILES], U32))
        weights = ctx.enter_context(nc.sbuf_tensor("weights", [P, CHOICES, TILES], F32))
        with ExitStack() as inner:
            cT = inner.enter_context(nc.sbuf_tensor("cT", [P, 2, TOKENS], F32))
            tile_expert = inner.enter_context(nc.sbuf_tensor("tile_expert", [1, SLOT_TILES], mybir.dt.int32))
            phase_norm(nc, x, wdq, wdkv, wuv, router, ln_scale, ln_bias, identity, iota, earlier, iota_tiles,
                       v_scratch, xn_scratch, acc_scratch, slot_rows, cT, slots, weights, tile_expert)
            phase_experts(nc, w_gu, w_dn, w_qk, cos_t, sin_t, identity, xn_scratch, slot_rows, y_rows, qk_scratch,
                          cT, slots, tile_expert)
        phase_attention(nc, identity, w_out, qk_scratch, v_scratch, acc_scratch, y_rows, slots, weights, out)


def rotary_tables():
    inv_freq = 1.0 / 10000.0 ** (np.arange(0, DH, 2, dtype=np.float32) / DH)
    freqs = np.outer(np.arange(S, dtype=np.float32), inv_freq)
    cos = np.concatenate([np.cos(freqs), np.cos(freqs)], -1)[:, ::2]
    sin = np.concatenate([np.sin(freqs), np.sin(freqs)], -1)[:, ::2]
    c, s = cos.T.astype(np.float32), sin.T.astype(np.float32)
    return np.concatenate([c, c, c, c]), np.concatenate([-s, s, -s, s])


def kernel(**inputs):
    import concourse.bacc as _bacc
    from concourse.bass_utils import run_bass_kernel_spmd as _run

    a = {n.removeprefix("L0_"): np.asarray(v) for n, v in inputs.items()}

    def rows_of_heads(w, flip):
        r = w.reshape(H // 2, 2, DH // 2, 2, LATENT)
        r = r[:, :, :, ::-1] if flip else r
        return r.transpose(0, 4, 1, 3, 2).reshape(H // 2, LATENT, P)

    up_q, up_k = a["attn_w_up_q"], a["attn_w_up_k"]
    cos_t, sin_t = rotary_tables()
    arrays = {
        "x": a["attn_x"].reshape(TOKENS, D),
        "wdq": a["attn_w_down_q"].T,
        "wdkv": a["attn_w_down_kv"].T,
        "w_qk": np.stack([rows_of_heads(w, f) for w in (up_q, up_k) for f in (False, True)], axis=2),
        "wuv": a["attn_w_up_v"].T,
        "w_out": a["attn_w_out"].T,
        "ln_scale": a["attn_ln_scale"].reshape(KD, P).T,
        "ln_bias": a["attn_ln_bias"].reshape(KD, P).T,
        "router": a["ffn_router_w"],
        "w_gu": a["ffn_w_gate_up"].reshape(E, KD, P, 2 * F).transpose(2, 0, 1, 3),
        "w_dn": a["ffn_w_down"].reshape(E, F // P, P, D).transpose(2, 0, 1, 3),
        "identity": np.eye(P, dtype=np.float32),
        "iota": np.tile(np.arange(E, dtype=np.float32), (P, 1)),
        "earlier": np.triu(np.ones((P, P), np.float32), 1),
        "iota_tiles": np.repeat(np.arange(SLOT_TILES, dtype=np.float32), E)[None],
        "cos_t": cos_t,
        "sin_t": sin_t,
    }
    nc = _bacc.Bacc("TRN2", target_bir_lowering=False, num_devices=1)
    feeds, args = {}, []
    for name, array in arrays.items():
        feeds[f"in_{name}"] = np.ascontiguousarray(array)
        args.append(nc.dram_tensor(f"in_{name}", array.shape, F32, kind="ExternalInput").ap())
    args.append(nc.dram_tensor("out_0", (TOKENS, D), F32, kind="ExternalOutput").ap())
    program(nc, *args)
    r = _run(nc, [feeds], core_ids=[0])
    return r.results[0]["out_0"].reshape(B, S, D)
```

```python
from contextlib import ExitStack

import concourse.bass as bass
import numpy as np
from concourse import mybir

ALU = mybir.AluOpType
ACT = mybir.ActivationFunctionType
AX = mybir.AxisListType
F32 = mybir.dt.float32
F32R = mybir.dt.float32r
U32 = mybir.dt.uint32

P = 128
B, S, D = 2, 2048, 256
H, DH = 16, 64
E, F = 16, 256
LATENT = 128
TOKENS = B * S
TILES = TOKENS // P
CH = 512
CT = CH // P
KD = D // P
KT = S // P
QC = S // CH
EPS = 1e-5
SCALE = 1.0 / 8.0
PAIRS = B * H // 2
CHOICES = 2
SLOT_TILES = 80
assert SLOT_TILES >= CHOICES * TOKENS // P + E - 1


def need(eng, semaphore, value):
    if isinstance(value, int) and value <= 0:
        return
    eng.wait_ge(semaphore, value)


def within(n, total):
    return not isinstance(n, int) or 0 <= n < total


class Memory:

    def __init__(self, nc, ctx):
        self.nc, self.ctx = nc, ctx

    def sb(self, name, shape, dtype=F32):
        return self.ctx.enter_context(self.nc.sbuf_tensor(name, shape, dtype))

    def bank(self, name):
        return self.ctx.enter_context(self.nc.psum_tensor(name, [P, CH], F32))

    def sem(self, name):
        return self.ctx.enter_context(self.nc.semaphore(name))


def phase_norm(nc, x, wdq, wdkv, wuv, router, ln_scale, ln_bias, identity, iota, earlier, iota_tiles,
               v_scratch, xn_scratch, acc_scratch, slot_rows, cT, slots, weights, tile_expert):
    chunks = TOKENS // CH
    with ExitStack() as ctx:
        m = Memory(nc, ctx)
        x_in = [m.sb(f"x_in{u}", [P, CT, D]) for u in range(2)]
        xn = [m.sb(f"xn{u}", [P, CT, D]) for u in range(2)]
        xn2 = [m.sb(f"xn2_{u}", [P, CT, D]) for u in range(2)]
        stats = m.sb("stats", [P, 2, CT, 6])
        moments = m.sb("moments", [P, 2, CT, 2])
        var_eps = m.sb("var_eps", [P, 2, CT])
        minus_half = m.sb("minus_half", [P, CT])
        rstd = m.sb("rstd", [P, 2, CT])
        xnT_c = [m.sb(f"xnT_c{u}", [P, KD, CH]) for u in range(2)]
        hT_c = [m.sb(f"hT_c{u}", [P, KD, CH]) for u in range(2)]
        c_c = [m.sb(f"c_c{u}", [P, 2, CH]) for u in range(2)]
        v_c = [m.sb(f"v_c{u}", [P, H, CT, DH]) for u in range(2)]
        logits = m.sb("logits", [P, TILES, E])
        wdq_sb = m.sb("wdq_sb", [P, KD, LATENT])
        wdkv_sb = m.sb("wdkv_sb", [P, KD, LATENT])
        wuv_sb = m.sb("wuv_sb", [P, H * DH])
        router_sb = m.sb("router_sb", [P, KD, E])
        res_c = [m.sb(f"res_c{u}", [P, CT, D]) for u in range(2)]
        EMPTY = SLOT_TILES // chunks
        zeros = m.sb("zeros", [P, EMPTY * D])
        earlier_sb = m.sb("earlier_sb", [P, P])
        all_ones = m.sb("all_ones", [P, P])
        iota_tiles_sb = m.sb("iota_tiles_sb", [1, SLOT_TILES * E])
        scale_sb = m.sb("scale_sb", [P, KD])
        bias_sb = m.sb("bias_sb", [P, KD])
        ident = m.sb("ident", [P, P])
        iota_sb = m.sb("iota_sb", [P, E])
        top = m.sb("top", [P, TILES, 8])
        top_at = m.sb("top_at", [P, TILES, 8], U32)
        top_atf = m.sb("top_atf", [P, TILES, 2])
        gap = m.sb("gap", [P, TILES])
        ratio = m.sb("ratio", [P, TILES])
        denom = m.sb("denom", [P, TILES])
        chosen = [m.sb(f"chosen{n}", [P, TILES, E]) for n in range(CHOICES)]
        both = m.sb("both", [P, TILES, E])
        totals = m.sb("totals", [P, TILES, E])
        upto = [m.sb(f"upto{n}", [P, TILES, E]) for n in range(2)]
        picked = [m.sb(f"picked{n}", [P, TILES, E]) for n in range(CHOICES)]
        slots_f = m.sb("slots_f", [P, CHOICES, TILES])
        tiles_i = m.sb("tiles_i", [P, E], mybir.dt.int32)
        tiles_f = m.sb("tiles_f", [P, E])
        ends = [m.sb(f"ends{n}", [P, E]) for n in range(2)]
        starts = m.sb("starts", [P, E])
        past = m.sb("past", [1, SLOT_TILES, E])
        expert_f = m.sb("expert_f", [1, SLOT_TILES])
        t_bank = [m.bank(f"t_bank{n}") for n in range(4)]
        c_bank = [m.bank(f"c_bank{n}") for n in range(2)]
        v_bank = [m.bank(f"v_bank{n}") for n in range(2)]

        weights_in = m.sem("weights_in")
        x_loaded = [m.sem(f"x_loaded{u}") for u in range(2)]
        norm1 = m.sem("norm1")
        norm2 = m.sem("norm2")
        small = m.sem("small")
        half_set = m.sem("half_set")
        passed = m.sem("passed")
        rstd_set = m.sem("rstd_set")
        turned = m.sem("turned")
        evac_x = m.sem("evac_x")
        evac_h = m.sem("evac_h")
        latent = m.sem("latent")
        latent_out = m.sem("latent_out")
        v_done = m.sem("v_done")
        v_out = m.sem("v_out")
        routed = m.sem("routed")
        routed_out = m.sem("routed_out")
        acc_set = m.sem("acc_set")
        kept_x = [m.sem(f"kept_x{u}") for u in range(2)]
        kept_r = [m.sem(f"kept_r{u}") for u in range(2)]
        kept_v = [m.sem(f"kept_v{u}") for u in range(2)]
        gap_set = m.sem("gap_set")
        ratio_set = m.sem("ratio_set")
        route = m.sem("route")
        counted = m.sem("counted")
        zeros_set = m.sem("zeros_set")
        cleared = m.sem("cleared")

        block = ctx.enter_context(nc.Block())
        x_t = x.rearrange("(m j p) d -> m p j d", p=P, j=CT)
        BOTH_SET = 9
        VN = 2 * CT

        def rolled(eng, step):
            for n in range(4):
                step(n // 2, n % 2)
            with eng.Fori(2, chunks // 2) as i:
                for u in range(2):
                    step(i, u)
            step(chunks // 2, 0)

        def previous(i, u):
            return (i, 0) if u == 1 else (i - 1, 1)

        @block.sync
        def _(sp):
            def load(i, u):
                sp.dma_start(x_in[u][:, :, :], x_t[2 * i + u]).then_inc(x_loaded[u], 16)

            load(0, 0)
            load(0, 1)
            sp.dma_start(ident[:, :], identity).then_inc(weights_in, 16)
            sp.dma_start(scale_sb[:, :], ln_scale).then_inc(weights_in, 16)
            sp.dma_start(bias_sb[:, :], ln_bias).then_inc(weights_in, 16)
            sp.dma_start(wdq_sb[:, :, :], wdq.rearrange("(k p) c -> p k c", p=P)).then_inc(weights_in, 16)
            sp.dma_start(wdkv_sb[:, :, :], wdkv.rearrange("(k p) c -> p k c", p=P)).then_inc(weights_in, 16)
            sp.dma_start(wuv_sb[:, :], wuv).then_inc(weights_in, 16)
            sp.dma_start(router_sb[:, :, :], router.rearrange("(k p) e -> p k e", p=P)).then_inc(weights_in, 16)
            sp.dma_start(iota_sb[:, :], iota).then_inc(weights_in, 16)
            sp.dma_start(earlier_sb[:, :], earlier).then_inc(weights_in, 16)
            sp.dma_start(iota_tiles_sb[:, :], iota_tiles).then_inc(weights_in, 16)

            def norms(i, u, more):
                n = 2 * i + u
                sp.wait_ge(norm1, CT * (n + 1))
                sp.sem_inc(passed, 1)
                sp.dma_start(xn_scratch[n].rearrange("(j p) d -> p j d", p=P), xn[u][:, :, :]).then_inc(kept_x[u], 16)
                sp.wait_ge(acc_set, n + 1)
                sp.sem_inc(passed, 1)
                sp.dma_start(acc_scratch[:, bass.ds(CT * n, CT), :], res_c[u][:, :, :]).then_inc(kept_r[u], 16)
                if more:
                    load(i + 1, u)

            def products(i, u):
                n = 2 * i + u
                sp.wait_ge(latent_out, 2 * (n + 1))
                sp.sem_inc(passed, 1)
                sp.dma_start(cT[:, :, bass.ds(CH * n, CH)], c_c[u][:, :, :]).then_inc(kept_v[u], 16)
                sp.wait_ge(v_out, VN * (n + 1))
                sp.sem_inc(passed, 1)
                sp.dma_start(v_scratch[n], v_c[u][:, :, :, :]).then_inc(kept_v[u], 16)

            norms(0, 0, True)
            norms(0, 1, True)
            products(0, 0)
            with sp.Fori(1, chunks // 2 - 1) as i:
                for u in range(2):
                    norms(i, u, True)
                    products(*previous(i, u))
            for u in range(2):
                norms(chunks // 2 - 1, u, False)
                products(*previous(chunks // 2 - 1, u))
            products(chunks // 2 - 1, 1)
            for u in range(2):
                sp.wait_ge(kept_x[u], 16 * (chunks // 2))
                sp.wait_ge(kept_r[u], 16 * (chunks // 2))
                sp.wait_ge(kept_v[u], 32 * (chunks // 2))

        @block.vector
        def _(dve):
            STEPS = 2 * (2 * CT + 1)

            def norm(i, u, which, src, dst, done):
                n = 2 * i + u
                base = STEPS * n + which * (2 * CT + 1)
                for j in range(CT):
                    nc.vector.bn_stats(stats[:, which, j, :], src[:, j, :]).then_inc(small, 1)
                dve.wait_ge(small, base + CT)
                dve.sem_inc(passed, 1)
                for j in range(CT):
                    nc.vector.bn_aggr(moments[:, which, j, :], stats[:, which, j, :]).then_inc(small, 1)
                dve.wait_ge(small, base + 2 * CT)
                nc.vector.tensor_scalar(var_eps[:, which, :], moments[:, which, :, 1], EPS, None,
                                        ALU.add).then_inc(small, 1)
                dve.wait_ge(rstd_set, 2 * n + which + 1)
                for j in range(CT):
                    nc.vector.tensor_scalar(dst[:, j, :], src[:, j, :], moments[:, which, j, 0:1],
                                            rstd[:, which, j:j + 1], ALU.subtract, ALU.mult).then_inc(done, 1)

            def step(i, u):
                n = 2 * i + u
                if within(n, chunks):
                    dve.wait_ge(x_loaded[u], 16 * (i + 1))
                    need(dve, turned, 4 * (n - 1))
                    need(dve, acc_set, n - 1)
                    need(dve, kept_x[u], 16 * i)
                    norm(i, u, 0, x_in[u], xn[u], norm1)
                    dve.wait_ge(norm1, CT * (n + 1))
                    norm(i, u, 1, xn[u], xn2[u], norm2)
                    if isinstance(n, int) and n == 0:
                        dve.wait_ge(weights_in, 16 * 10)
                    need(dve, latent, 2 * (n - 1))
                    for k in range(KD):
                        dve.wait_ge(turned, 4 * n + 3 + k)
                        nc.vector.tensor_scalar(hT_c[u][:, k, :], t_bank[2 + k][:, :], scale_sb[:, k:k + 1],
                                                bias_sb[:, k:k + 1], ALU.mult, ALU.add).then_inc(evac_h, 1)
                if within(n - 1, chunks):
                    dve.wait_ge(routed, n)
                    nc.vector.tensor_copy(logits[:, bass.ds(CT * (n - 1), CT), :],
                                          c_bank[0][:, 0:CT * E].rearrange("p (j e) -> p j e", e=E)).then_inc(routed_out, 1)

            rolled(dve, step)

            step = [0]

            def link(ins):
                step[0] += 1
                ins.then_inc(route, 1)
                dve.wait_ge(route, step[0])

            dve.wait_ge(routed_out, chunks)
            for t in range(TILES):
                ins = nc.vector.max(top[:, t, :], logits[:, t, :])
                link(ins) if t == TILES - 1 else None
            for t in range(TILES):
                ins = nc.vector.max_index(top_at[:, t, :], top[:, t, :], logits[:, t, :])
            link(ins)
            nc.vector.tensor_tensor(gap[:, :], top[:, :, 1], top[:, :, 0], ALU.subtract).then_inc(gap_set, 1)
            link(nc.vector.tensor_copy(top_atf[:, :, :], top_at[:, :, 0:CHOICES]))
            dve.wait_ge(ratio_set, 1)
            link(nc.vector.tensor_scalar(denom[:, :], ratio[:, :], 1.0, None, ALU.add))
            link(nc.vector.reciprocal(weights[:, 0, :], denom[:, :]))
            link(nc.vector.tensor_tensor(weights[:, 1, :], weights[:, 0, :], ratio[:, :], ALU.mult))

            full = [P, TILES, E]
            for n in range(CHOICES):
                link(nc.vector.tensor_tensor(chosen[n][:, :, :], iota_sb[:, :].unsqueeze(1).broadcast_to(full),
                                             top_atf[:, :, n:n + 1].broadcast_to(full), ALU.is_equal))
            link(nc.vector.tensor_tensor(both[:, :, :], chosen[0][:, :, :], chosen[1][:, :, :], ALU.add))
            both_set = step[0]
            assert both_set == BOTH_SET
            dve.wait_ge(counted, 2)
            flat = "p (t e) -> p t e"
            link(nc.vector.tensor_copy(totals[:, :, :], t_bank[1][:, :].rearrange(flat, e=E)))
            source, at, by = totals, 0, 1
            while by < TILES:
                link(nc.vector.tensor_copy(upto[at][:, 0:by, :], source[:, 0:by, :]))
                link(nc.vector.tensor_tensor(upto[at][:, by:, :], source[:, by:, :], source[:, 0:TILES - by, :], ALU.add))
                source, at, by = upto[at], 1 - at, 2 * by
            count = source[:, TILES - 1, :]
            link(nc.vector.tensor_scalar(tiles_f[:, :], count, float(P - 1), None, ALU.add))
            link(nc.vector.tensor_copy(tiles_i[:, :], tiles_f[:, :]))
            link(nc.vector.tensor_scalar(tiles_i[:, :], tiles_i[:, :], 7, None, ALU.logical_shift_right))
            link(nc.vector.tensor_copy(tiles_f[:, :], tiles_i[:, :]))
            end, to, by = tiles_f, 0, 1
            while by < E:
                link(nc.vector.tensor_copy(ends[to][:, 0:by], end[:, 0:by]))
                link(nc.vector.tensor_tensor(ends[to][:, by:], end[:, by:], end[:, 0:E - by], ALU.add))
                end, to, by = ends[to], 1 - to, 2 * by
            link(nc.vector.tensor_tensor(starts[:, :], end[:, :], tiles_f[:, :], ALU.subtract))
            link(nc.vector.tensor_scalar(starts[:, :], starts[:, :], float(P), None, ALU.mult))

            link(nc.vector.tensor_tensor(source[:, :, :], source[:, :, :], totals[:, :, :], ALU.subtract))
            link(nc.vector.tensor_tensor(source[:, :, :], t_bank[0][:, :].rearrange(flat, e=E), source[:, :, :], ALU.add))
            link(nc.vector.tensor_tensor(source[:, :, :], source[:, :, :], starts[:, :].unsqueeze(1).broadcast_to(full), ALU.add))
            for n in range(CHOICES):
                link(nc.vector.tensor_tensor(picked[n][:, :, :], source[:, :, :], chosen[n][:, :, :], ALU.mult))
                link(nc.vector.tensor_reduce(slots_f[:, n, :], picked[n][:, :, :], AX.X, ALU.add))
            link(nc.vector.tensor_copy(slots[:, :, :], slots_f[:, :, :]))

            tiles_by_e = [1, SLOT_TILES, E]
            link(nc.vector.tensor_tensor(past[:, :, :], iota_tiles_sb[:, :].rearrange(flat, e=E),
                                         end[0:1, :].unsqueeze(1).broadcast_to(tiles_by_e), ALU.is_ge))
            link(nc.vector.tensor_reduce(expert_f[:, :], past[:, :, :], AX.X, ALU.add))
            link(nc.vector.tensor_scalar(expert_f[:, :], expert_f[:, :], float(E - 1), None, ALU.min))
            link(nc.vector.tensor_copy(tile_expert[:, :], expert_f[:, :]))

        @block.scalar
        def _(act):
            def step(i, u):
                n = 2 * i + u
                if within(n - 1, chunks):
                    i1, v = previous(i, u)
                    need(act, kept_v[v], 32 * i1)
                    need(act, v_done, VN * (n - 2))
                    for k in range(2):
                        act.wait_ge(latent, 2 * (n - 1) + 1 + k)
                        nc.scalar.activation(c_c[v][:, k, :], c_bank[k][:, :], ACT.Copy).then_inc(latent_out, 1)
                if within(n, chunks):
                    need(act, routed, n - 1)
                    for k in range(KD):
                        act.wait_ge(turned, 4 * n + 1 + k)
                        nc.scalar.activation(xnT_c[u][:, k, :], t_bank[k][:, :], ACT.Copy).then_inc(evac_x, 1)
                    act.dma_start(slot_rows.rearrange("(m p t) d -> m p (t d)", p=P, t=EMPTY)[n], zeros[:, :]).then_inc(cleared, 16)
                if within(n - 1, chunks):
                    for j in range(CT):
                        for half in range(2):
                            act.wait_ge(v_done, VN * (n - 1) + 2 * j + half + 1)
                            nc.scalar.activation(v_c[v][:, H // 2 * half:H // 2 * (half + 1), j, :],
                                                 v_bank[half][:, :].rearrange("p (h d) -> p h d", d=DH), ACT.Copy).then_inc(v_out, 1)

            act.wait_ge(zeros_set, 1)
            rolled(act, step)
            act.wait_ge(gap_set, 1)
            nc.scalar.activation(ratio[:, :], gap[:, :], ACT.Exp).then_inc(ratio_set, 1)
            act.wait_ge(cleared, 16 * chunks)

        @block.gpsimd
        def _(pool):
            def step(i, u):
                n = 2 * i + u
                if not within(n, chunks):
                    return
                for which in range(2):
                    pool.wait_ge(small, (4 * CT + 2) * n + (which + 1) * (2 * CT + 1))
                    nc.gpsimd.tensor_tensor(rstd[:, which, :], var_eps[:, which, :], minus_half[:, :], ALU.pow
                                            ).then_inc(rstd_set, 1)
                pool.wait_ge(norm1, CT * (n + 1))
                need(pool, kept_r[u], 16 * i)
                nc.gpsimd.tensor_tensor(res_c[u][:, :, :], x_in[u][:, :, :], xn[u][:, :, :],
                                        ALU.add).then_inc(acc_set, 1)

            nc.gpsimd.memset(minus_half[:, :], -0.5).then_inc(half_set, 1)
            nc.gpsimd.memset(all_ones[:, :], 1.0).then_inc(half_set, 1)
            nc.gpsimd.memset(zeros[:, :], 0.0).then_inc(zeros_set, 1)
            pool.wait_ge(half_set, 2)
            rolled(pool, step)

        @block.tensor
        def _(pe):
            pe.wait_ge(weights_in, 16 * 10)

            def step(i, u):
                n = 2 * i + u
                _, v = previous(i, u)
                if within(n - 1, chunks):
                    need(pe, routed_out, n - 1)
                    pe.wait_ge(evac_h, KD * n)
                    for c, w in enumerate((wdq_sb, wdkv_sb)):
                        for k in range(KD):
                            mm = nc.tensor.matmul(c_bank[c][:, :], w[:, k, :], hT_c[v][:, k, :], start=(k == 0), stop=(k == KD - 1))
                        mm.then_inc(latent, 1)
                if within(n, chunks):
                    for which, (src, done, evac) in enumerate(((xn[u], norm1, evac_x), (xn2[u], norm2, evac_h))):
                        pe.wait_ge(done, CT * (n + 1))
                        for k in range(KD):
                            need(pe, evac, KD * (n - 1) + k + 1)
                            for j in range(CT):
                                mm = nc.tensor.transpose(t_bank[2 * which + k][:, j * P:(j + 1) * P],
                                                         src[:, j, k * P:(k + 1) * P], ident[:, :])
                            mm.then_inc(turned, 1)
                if within(n - 1, chunks):
                    pe.wait_ge(latent_out, 2 * n)
                    pe.wait_ge(evac_x, KD * n)
                    for j in range(CT):
                        for k in range(KD):
                            mm = nc.tensor.matmul(c_bank[0][:, j * E:(j + 1) * E], xnT_c[v][:, k, j * P:(j + 1) * P],
                                                  router_sb[:, k, :], start=(k == 0), stop=(k == KD - 1))
                    mm.then_inc(routed, 1)
                    for j in range(CT):
                        for half in range(2):
                            need(pe, v_out, VN * (n - 1) + 2 * (j - 1) + half + 1)
                            nc.tensor.matmul(v_bank[half][:, :], c_c[v][:, 1, j * P:(j + 1) * P],
                                             wuv_sb[:, half * CH:(half + 1) * CH], start=True, stop=True).then_inc(v_done, 1)

            rolled(pe, step)
            pe.wait_ge(half_set, 2)
            pe.wait_ge(route, BOTH_SET)
            for n, w in enumerate((earlier_sb, all_ones)):
                nc.tensor.matmul(t_bank[n][:, :], w[:, :], both[:, :, :].rearrange("p t e -> p (t e)"), start=True, stop=True
                                 ).then_inc(counted, 1)


def phase_experts(nc, w_gu, w_dn, w_qk, cos_t, sin_t, identity, xn_scratch, slot_rows, y_rows, qk_scratch,
                  cT, slots, tile_expert):
    PER = 16
    STEPS = PAIRS * 8
    FIRST = STEPS - SLOT_TILES
    assert FIRST == 3 * PER and SLOT_TILES % PER == 0 and E == PER
    with ExitStack() as ctx:
        m = Memory(nc, ctx)
        gu_sb = m.sb("gu_sb", [P, E, KD, 2 * F])
        dn_sb = m.sb("dn_sb", [P, E, F // P, D])
        qk_sb = [m.sb(f"qk_sb{u}", [P, 4, P]) for u in range(2)]
        ident = m.sb("ident2", [P, P])
        cos_sb = m.sb("cos_sb", [P, S])
        sin_sb = m.sb("sin_sb", [P, S])
        by_cos = [m.sb(f"by_cos{u}", [P, CH]) for u in range(2)]
        by_sin = [m.sb(f"by_sin{u}", [P, CH]) for u in range(2)]
        rot = [m.sb(f"rot{u}", [P, CH]) for u in range(2)]
        hi = [m.sb(f"hi{u}", [P, CH], F32R) for u in range(2)]
        lo = [m.sb(f"lo{u}", [P, CH], F32R) for u in range(2)]
        STAGES = 2
        stage = [m.sb(f"stage{n}", [P, CT, D]) for n in range(STAGES)]
        rows = [m.sb(f"rows{u}", [P, D]) for u in range(2)]
        rowsT = [m.sb(f"rowsT{u}", [P, KD, P]) for u in range(2)]
        silu = [m.sb(f"silu{u}", [P, F]) for u in range(2)]
        gated = [m.sb(f"gated{u}", [P, F]) for u in range(2)]
        gatedT = [m.sb(f"gatedT{u}", [P, F // P, P]) for u in range(2)]
        y = [m.sb(f"y{u}", [P, D]) for u in range(2)]
        pr_bank = [m.bank(f"pr_bank{n}") for n in range(2)]
        xt_bank = m.bank("xt_bank")
        gu_bank = [m.bank(f"gu_bank{n}") for n in range(2)]
        gt_bank = m.bank("gt_bank")
        y_bank = m.bank("y_bank")

        tables_in = m.sem("tables_in")
        experts_in = m.sem("experts_in")
        passed2 = m.sem("passed2")
        w_in = [m.sem(f"w_in{u}") for u in range(2)]
        pr_done = m.sem("pr_done")
        mul_done = m.sem("mul_done")
        rot_done = m.sem("rot_done")
        hi_done = m.sem("hi_done")
        lo_done = m.sem("lo_done")
        stored = [m.sem(f"stored{u}") for u in range(2)]
        staged = [m.sem(f"staged{n}") for n in range(STAGES)]
        scattered = [m.sem(f"scattered{n}") for n in range(STAGES)]
        rows_in = [m.sem(f"rows_in{u}") for u in range(2)]
        xt_done = m.sem("xt_done")
        xt_set = m.sem("xt_set")
        g_done = m.sem("g_done")
        silu_done = m.sem("silu_done")
        gated_set = m.sem("gated_set")
        gt_done = m.sem("gt_done")
        gt_set = m.sem("gt_set")
        y_done = m.sem("y_done")
        y_set = m.sem("y_set")
        y_kept = [m.sem(f"y_kept{u}") for u in range(2)]

        block = ctx.enter_context(nc.Block())

        def rolled(eng, step):
            def turn(i, tiles):
                for j in range(PER):
                    step(PER * i + j, i, j, tiles)
            turn(0, False)
            with eng.Fori(1, FIRST // PER) as i:
                turn(i, False)
            turn(FIRST // PER, True)
            with eng.Fori(FIRST // PER + 1, STEPS // PER - 1) as i:
                turn(i, True)
            turn(STEPS // PER - 1, True)
            for j in range(3):
                step(STEPS + j, STEPS // PER, j, True)

        def uses(i, j):
            return PER // 2 * i + j // 2 - FIRST // 2

        @block.sync
        def _(sp):
            def load_pair(pair, u):
                sp.dma_start(qk_sb[u][:, :, :], w_qk[pair % (H // 2)]).then_inc(w_in[u], 16)

            def load_rows(f, i, j):
                need(sp, xt_done, f - 1)
                sp.dma_start(rows[j % 2][:, :], slot_rows.rearrange("(t p) d -> t p d", p=P)[f]).then_inc(rows_in[j % 2], 16)

            load_pair(0, 0)
            sp.dma_start(cos_sb[:, :], cos_t).then_inc(tables_in, 16)
            sp.dma_start(sin_sb[:, :], sin_t).then_inc(tables_in, 16)
            sp.dma_start(ident[:, :], identity).then_inc(tables_in, 16)

            def step(s, i, j, tiles):
                u = j // 8 % 2
                f = s - FIRST
                if tiles and isinstance(f, int) and f == 0:
                    for n in range(STAGES):
                        sp.wait_ge(scattered[n], 16 * CHOICES * TILES // STAGES)
                    load_rows(0, i, j)
                    load_rows(1, i, j + 1)
                if within(s, STEPS):
                    if j % 8 == 2 and (not isinstance(i, int) or 2 * i + u + 1 < PAIRS):
                        need(sp, pr_done, 16 * (2 * i + u))
                        sp.sem_inc(passed2, 1)
                        load_pair(2 * i + u + 1, 1 - u)
                    at = slice(CH * (j % 4), CH * (j % 4 + 1))
                    sp.wait_ge(hi_done, s + 1)
                    sp.dma_start(qk_scratch[2 * i + u][:, 2 * (j % 8 // 4), at], hi[j % 2][:, :].bitcast(F32)).then_inc(stored[j % 2], 16)
                    sp.wait_ge(lo_done, s + 1)
                    sp.dma_start(qk_scratch[2 * i + u][:, 2 * (j % 8 // 4) + 1, at], lo[j % 2][:, :].bitcast(F32)).then_inc(stored[j % 2], 16)
                if tiles and within(f, SLOT_TILES) and within(f + 2, SLOT_TILES):
                    load_rows(f + 2, i, j)
                if tiles and within(f - 3, SLOT_TILES):
                    sp.wait_ge(y_set, f - 2)
                    sp.dma_start(y_rows.rearrange("(t p) d -> t p d", p=P)[f - 3], y[(j - 3) % 2][:, :]).then_inc(y_kept[(j - 3) % 2], 16)

            rolled(sp, step)
            for u in range(2):
                sp.wait_ge(stored[u], 32 * (STEPS // 2))
                sp.wait_ge(y_kept[u], 16 * (SLOT_TILES // 2))

        @block.tensor
        def _(pe):
            def step(s, i, j, tiles):
                u = j // 8 % 2
                f = s - FIRST
                if tiles and within(f - 1, SLOT_TILES):
                    gu_expert = pe.value_load(tile_expert[0:1, bass.ds(f - 1, 1)], min_val=0, max_val=E - 1)
                if tiles and within(f - 3, SLOT_TILES):
                    dn_expert = pe.value_load(tile_expert[0:1, bass.ds(f - 3, 1)], min_val=0, max_val=E - 1)
                if within(s, STEPS):
                    if j % 8 == 0:
                        pe.wait_ge(w_in[u], 16 * (i + 1))
                    sequence = (2 * i + u) // (H // 2)
                    for n in range(2):
                        need(pe, mul_done, 2 * (s - 1) + n + 1)
                        nc.tensor.matmul(pr_bank[n][:, :], qk_sb[u][:, 2 * (j % 8 // 4) + n, :],
                                         cT[:, j % 8 // 4, bass.ds(S * sequence + CH * (j % 4), CH)],
                                         start=True, stop=True).then_inc(pr_done, 1)
                if not tiles:
                    return
                if within(f, SLOT_TILES):
                    pe.wait_ge(tables_in, 48)
                    pe.wait_ge(rows_in[j % 2], 16 * (uses(i, j) + 1))
                    need(pe, xt_set, f)
                    for k in range(KD):
                        mm = nc.tensor.transpose(xt_bank[:, P * k:P * (k + 1)], rows[j % 2][:, P * k:P * (k + 1)], ident[:, :])
                    mm.then_inc(xt_done, 1)
                if within(f - 2, SLOT_TILES):
                    pe.wait_ge(gated_set, f - 1)
                    need(pe, gt_set, f - 2)
                    for k in range(F // P):
                        mm = nc.tensor.transpose(gt_bank[:, P * k:P * (k + 1)], gated[j % 2][:, P * k:P * (k + 1)], ident[:, :])
                    mm.then_inc(gt_done, 1)
                if within(f - 1, SLOT_TILES):
                    pe.wait_ge(experts_in, 32 * E)
                    pe.wait_ge(xt_set, f)
                    need(pe, gated_set, f - 2)
                    for k in range(KD):
                        mm = nc.tensor.matmul(gu_bank[(j - 1) % 2][:, :], rowsT[(j - 1) % 2][:, k, :],
                                              gu_sb[:, bass.ds(gu_expert, 1), k, :].rearrange("p e f -> p (e f)"),
                                              start=(k == 0), stop=(k == KD - 1))
                    mm.then_inc(g_done, 1)
                if within(f - 3, SLOT_TILES):
                    pe.wait_ge(gt_set, f - 2)
                    need(pe, y_set, f - 3)
                    for k in range(F // P):
                        mm = nc.tensor.matmul(y_bank[:, 0:D], gatedT[(j - 3) % 2][:, k, :],
                                              dn_sb[:, bass.ds(dn_expert, 1), k, :].rearrange("p e d -> p (e d)"),
                                              start=(k == 0), stop=(k == F // P - 1))
                    mm.then_inc(y_done, 1)

            rolled(pe, step)

        @block.scalar
        def _(act):
            act.wait_ge(tables_in, 48)
            act.wait_ge(w_in[0], 16)

            def step(s, i, j, tiles):
                f = s - FIRST
                if not tiles and (not isinstance(i, int) or i > 0) and j % 2 == 0:
                    e = PER // 2 * (i - 1) + j // 2
                    act.dma_start(gu_sb[:, bass.ds(e, 1), :, :], w_gu[:, bass.ds(e, 1), :, :]).then_inc(experts_in, 16)
                    act.dma_start(dn_sb[:, bass.ds(e, 1), :, :], w_dn[:, bass.ds(e, 1), :, :]).then_inc(experts_in, 16)
                if within(s - 1, STEPS):
                    v = (j - 1) % 2
                    act.wait_ge(rot_done, s)
                    need(act, lo_done, s - 2)
                    need(act, stored[v], 32 * (8 * i + (j - 1) // 2))
                    nc.scalar.activation(hi[v][:, :], rot[v][:, :], ACT.Copy).then_inc(hi_done, 1)
                if tiles and within(f - 2, SLOT_TILES):
                    act.wait_ge(gt_done, f - 1)
                    need(act, y_done, f - 3)
                    nc.scalar.activation(gatedT[j % 2][:, :, :], gt_bank[:, 0:F].rearrange("p (k t) -> p k t", t=P), ACT.Copy).then_inc(gt_set, 1)
                if tiles and within(f - 1, SLOT_TILES):
                    act.wait_ge(g_done, f)
                    need(act, gated_set, f - 2)
                    nc.scalar.activation(silu[(j - 1) % 2][:, :], gu_bank[(j - 1) % 2][:, 0:F], ACT.Silu).then_inc(silu_done, 1)

            rolled(act, step)

        @block.vector
        def _(dve):
            dve.wait_ge(tables_in, 48)

            def step(s, i, j, tiles):
                f = s - FIRST
                if within(s, STEPS):
                    need(dve, rot_done, s - 1)
                    at = slice(CH * (j % 4), CH * (j % 4 + 1))
                    for n, (out, table) in enumerate(((by_cos[j % 2], cos_sb), (by_sin[j % 2], sin_sb))):
                        dve.wait_ge(pr_done, 2 * s + n + 1)
                        nc.vector.tensor_tensor(out[:, :], pr_bank[n][:, :], table[:, at], ALU.mult).then_inc(mul_done, 1)
                if within(s - 1, STEPS):
                    v = (j - 1) % 2
                    dve.wait_ge(hi_done, s)
                    need(dve, stored[v], 32 * (8 * i + (j - 1) // 2))
                    nc.vector.tensor_tensor(lo[v][:, :], rot[v][:, :], hi[v][:, :], ALU.subtract).then_inc(lo_done, 1)
                if tiles and within(f, SLOT_TILES):
                    dve.wait_ge(xt_done, f + 1)
                    need(dve, g_done, f - 1)
                    nc.vector.tensor_copy(rowsT[j % 2][:, :, :], xt_bank[:, 0:D].rearrange("p (k t) -> p k t", t=P)).then_inc(xt_set, 1)
                if within(s, STEPS):
                    dve.wait_ge(mul_done, 2 * (s + 1))
                    need(dve, lo_done, s - 1)
                    need(dve, hi_done, s - 1)
                    nc.vector.tensor_tensor(rot[j % 2][:, :], by_cos[j % 2][:, :], by_sin[j % 2][:, :], ALU.add).then_inc(rot_done, 1)
                if tiles and within(f - 1, SLOT_TILES):
                    dve.wait_ge(silu_done, f)
                    need(dve, gt_done, f - 2)
                    nc.vector.tensor_tensor(gated[(j - 1) % 2][:, :], silu[(j - 1) % 2][:, :], gu_bank[(j - 1) % 2][:, F:2 * F], ALU.mult
                                            ).then_inc(gated_set, 1)
                if tiles and within(f - 3, SLOT_TILES):
                    dve.wait_ge(y_done, f - 2)
                    need(dve, y_kept[(j - 3) % 2], 16 * uses(i, j - 3))
                    nc.vector.tensor_copy(y[(j - 3) % 2][:, :], y_bank[:, 0:D]).then_inc(y_set, 1)

            rolled(dve, step)

        @block.gpsimd
        def _(pool):
            def scatter(n):
                u = n % STAGES
                pool.wait_ge(staged[u], 16 * (n // STAGES + 1))
                for t in range(CT):
                    for choice in range(CHOICES):
                        at = CT * n + t
                        nc.gpsimd.indirect_dma_start(slot_rows, bass.IndirectOffsetOnAxis(ap=slots[:, choice, at:at + 1], axis=0),
                                                     stage[u][:, t, :], None).then_inc(scattered[u], 16)

            for n in range(TILES // CT):
                u = n % STAGES
                if n >= STAGES:
                    pool.wait_ge(scattered[u], 16 * CHOICES * CT * (n // STAGES))
                pool.dma_start(stage[u][:, :, :], xn_scratch[n].rearrange("(j p) d -> p j d", p=P)).then_inc(staged[u], 16)
                if n > 0:
                    scatter(n - 1)
            scatter(TILES // CT - 1)

def phase_attention(nc, identity, w_out, qk_scratch, v_scratch, acc_scratch, y_rows, slots, weights, out):
    CHUNKS = PAIRS * 8
    GROUPS = CHUNKS // 2
    PER = 16
    ST = 16
    Q_LOAD, K_LOAD, V_LOAD = 6 * 16, 4 * 16, 10 * 16
    ADDS = (5, 6)
    AFTER = ({0: 1, 1: 1, 3: 2, 4: 3, 5: 4, 7: 5}, {0: 1, 1: 2, 3: 3, 4: 4, 5: 5, 7: 6})
    with ExitStack() as ctx:
        m = Memory(nc, ctx)
        q_hh = [m.sb(f"q_hh{u}", [P, S], F32R) for u in range(2)]
        q_lm = [m.sb(f"q_lm{u}", [DH + 1, S], F32R) for u in range(2)]
        k_hl = [[m.sb(f"k_hl{w}{u}", [P, S], F32R) for u in range(2)] for w in range(2)]
        k_h1 = [[m.sb(f"k_h1{w}{u}", [DH + 1, S], F32R) for u in range(2)] for w in range(2)]
        v_sb = [[m.sb(f"v_sb{w}{u}", [P, KT, DH]) for u in range(2)] for w in range(2)]
        acc = m.sb("acc", [P, TILES, D])
        slot_now = [m.sb(f"slot_now{n}", [P, 1], U32) for n in range(CHOICES)]
        y_in = [m.sb(f"y_in{n}", [P, D]) for n in range(CHOICES)]
        w_out_sb = m.sb("w_out_sb", [P, H // 2, D])
        probs = m.sb("probs", [P, 8, CH])
        pair_sum = [m.sb(f"pair_sum{n}", [P, 2, CH]) for n in range(2)]
        sums = [m.sb(f"sums{n}", [P, 2, CH]) for n in range(2)]
        rsum = m.sb("rsum", [P, CH])
        normed = [m.sb(f"normed{n}", [P, CH]) for n in range(2)]
        maxes = [m.sb(f"maxes{n}", [P, CT, 4]) for n in range(2)]
        neg_max = [m.sb(f"neg_max{n}", [P, CT, DH + 1]) for n in range(2)]
        ident = m.sb("ident3", [P, P])
        ones_sb = m.sb("ones_sb", [P, DH])
        s_bank = [m.bank(f"s_bank{n}") for n in range(2)]
        a_bank = [m.bank(f"a_bank{n}") for n in range(2)]
        o_bank = [m.bank(f"o_bank{n}") for n in range(2)]
        m_bank = [m.bank(f"m_bank{n}") for n in range(2)]

        consts_in = m.sem("consts_in")
        consts_set = m.sem("consts_set")
        blank_set = m.sem("blank_set")
        q_in = [m.sem(f"q_in{n}") for n in range(QC)]
        k_in = [m.sem(f"k_in{w}") for w in range(2)]
        v_in = [m.sem(f"v_in{w}") for w in range(2)]
        s_done = m.sem("s_done")
        exp_done = m.sem("exp_done")
        a_done = m.sem("a_done")
        max_done = [m.sem(f"max_done{n}") for n in range(2)]
        negmax_set = m.sem("negmax_set")
        row_done = m.sem("row_done")
        row_set = m.sem("row_set")
        pv_done = m.sem("pv_done")
        pair_done = m.sem("pair_done")
        add_done = m.sem("add_done")
        l_done = m.sem("l_done")
        rsum_set = m.sem("rsum_set")
        norm_done = m.sem("norm_done")
        op_done = m.sem("op_done")
        acc_done3 = m.sem("acc_done3")
        out_done = m.sem("out_done")
        acc_in = m.sem("acc_in")
        slot_set = m.sem("slot_set")
        fetched = [m.sem(f"fetched{n}") for n in range(CHOICES)]
        passed3, passed4 = m.sem("passed3"), m.sem("passed4")
        mixed = m.sem("mixed")

        block = ctx.enter_context(nc.Block())

        def rolled(eng, chunk):
            def turn(i, cs):
                for c in cs:
                    chunk(PER * i + c, i, c)
            turn(-1, (PER - 3, PER - 2, PER - 1))
            turn(0, range(PER))
            with eng.Fori(1, CHUNKS // PER - 1) as i:
                turn(i, range(PER))
            turn(CHUNKS // PER - 1, range(PER))
            turn(CHUNKS // PER, (0, 1))

        def group(i, c):
            return PER // 2 * i + c // 2

        def ahead(i, c, n):
            return i + (c + n) // PER, (c + n) % PER

        def adds(i, c, n):
            return PER // 2 * sum(ADDS) * i + sum(ADDS) * (c // 2) + ADDS[0] * (c % 2) + AFTER[c % 2][n]

        @block.sync
        def _(sp):
            def load_q(pair, n):
                at = slice(CH * n, CH * (n + 1))
                for u in range(2):
                    src = qk_scratch[pair][DH * u:DH * (u + 1), :, at]
                    for dst, kind in ((q_hh[u][0:DH, at], 0), (q_hh[u][DH:P, at], 0), (q_lm[u][0:DH, at], 1)):
                        sp.dma_start(dst.bitcast(F32), src[:, kind, :]).then_inc(q_in[n], 16)

            def load_k(pair, w):
                for u in range(2):
                    src = qk_scratch[pair][DH * u:DH * (u + 1), :, :]
                    for half in range(2):
                        sp.dma_start(k_hl[w][u][DH * half:DH * (half + 1), :].bitcast(F32), src[:, 2 + half, :]).then_inc(k_in[w], 16)

            def load_v(pair, w):
                b, pair_of_b = pair // (H // 2), pair % (H // 2)
                for u in range(2):
                    sp.dma_start(k_h1[w][u][0:DH, :].bitcast(F32), qk_scratch[pair][DH * u:DH * (u + 1), 2, :]).then_inc(v_in[w], 16)
                    for c in range(QC):
                        sp.dma_start(v_sb[w][u][:, CT * c:CT * (c + 1), :],
                                     v_scratch[QC * b + c][:, bass.ds(2 * pair_of_b + u, 1), :, :].rearrange("p h j d -> p (h j) d")
                                     ).then_inc(v_in[w], 16)

            load_q(0, 0)
            load_k(0, 0)
            load_q(0, 1)
            sp.dma_start(ident[:, :], identity).then_inc(consts_in, 16)
            load_v(0, 0)
            sp.dma_start(w_out_sb[:, :, :], w_out.rearrange("(h p) n -> p h n", p=P)).then_inc(consts_in, 16)
            sp.dma_start(acc[:, :, :], acc_scratch).then_inc(acc_in, 16)
            for n in (2, 3):
                load_q(0, n)
            load_k(1, 1)
            load_v(1, 1)

            def turn(i, last):
                for w in range(2):
                    if last and w == 1:
                        return
                    for n in range(QC):
                        sp.wait_ge(s_done, 16 * (PER * i + 8 * w + 2 * n + 2))
                        sp.sem_inc(passed4, 1)
                        load_q(2 * i + w + 1, n)
                    if not last:
                        sp.wait_ge(pv_done, 4 * (PER * i + 8 * w + 8))
                        sp.sem_inc(passed4, 1)
                        load_k(2 * i + w + 2, w)
                        load_v(2 * i + w + 2, w)

            with sp.Fori(0, PAIRS // 2 - 1) as i:
                turn(i, False)
            turn(PAIRS // 2 - 1, True)
            sp.wait_ge(acc_done3, 2 * GROUPS)
            sp.wait_ge(mixed, CHUNKS // 2)
            sp.dma_start(out.rearrange("(t p) d -> p t d", p=P), acc[:, :, :]).then_inc(out_done, 16)
            sp.wait_ge(out_done, 16)

        @block.tensor
        def _(pe):
            def scores_T(k, i, c, n):
                w, u, q = c // 8, n % 2, CH * (c // 2 % QC)
                tile = 8 * (c % 2) + n // 2
                keys = slice(P * tile, P * (tile + 1))
                if n == 0 and c % 8 == 0:
                    pe.wait_ge(v_in[w], V_LOAD * (i + 1))
                if n == 0 and c % 2 == 0:
                    pe.wait_ge(row_set, k + 2)
                need(pe, exp_done, 16 * k + n - 1)
                nc.tensor.matmul(s_bank[n % 2][:, :], k_hl[w][u][:, keys], q_hh[u][:, q:q + CH], start=True, stop=False)
                nc.tensor.matmul(s_bank[n % 2][:, :], k_h1[w][u][:, keys], q_lm[u][:, q:q + CH], start=False, stop=True
                                 ).then_inc(s_done, 1)

            def scores(k, i, c, n):
                i, c = ahead(i, c, 3)
                w, u, slot = c // 8, c % 2, c // 2 % QC
                q = CH * slot + P * (n // 4)
                if n == 0 and c % 8 == 0:
                    pe.wait_ge(k_in[w], K_LOAD * (i + 1))
                if n == 0 and c % 2 == 0:
                    pe.wait_ge(q_in[slot], Q_LOAD * (2 * i + w + 1))
                need(pe, max_done[n % 2], 8 * (k + 3) + n // 2)
                nc.tensor.matmul(a_bank[n % 2][:, :], q_hh[u][:, q:q + P], k_hl[w][u][:, CH * (n % 4):CH * (n % 4 + 1)],
                                 start=True, stop=True).then_inc(a_done, 1)

            def values(k, i, c, r):
                if r == 0 and c % 2 == 0:
                    need(pe, norm_done, group(i, c) - 1)
                for n in range(4 * r, 4 * r + 4):
                    u = n % 2
                    if u == 0:
                        pe.wait_ge(exp_done, 16 * k + n + 2)
                    mm = nc.tensor.matmul(o_bank[c // 2 % 2][DH * u:DH * (u + 1), :], v_sb[c // 8][u][:, 8 * (c % 2) + n // 2, :],
                                          probs[:, n % 8, :], start=(c % 2 == 0 and n < 2), stop=(c % 2 == 1 and n >= ST - 2))
                mm.then_inc(pv_done, 1)

            def output(k, i, c):
                i, c = ahead(i, c, -3)
                pair = (2 * i + c // 8) % (H // 2)
                pe.wait_ge(norm_done, group(i, c) + 1)
                need(pe, row_set, min(k + 2, CHUNKS) if isinstance(k, int) else k + 2)
                for half in range(2):
                    for t in range(2):
                        tile = slice(P * (2 * half + t), P * (2 * half + t + 1))
                        mm = nc.tensor.matmul(m_bank[half][:, D * t:D * (t + 1)], normed[c // 2 % 2][:, tile],
                                              w_out_sb[:, bass.ds(pair, 1), :].rearrange("p h n -> p (h n)"), start=True, stop=True)
                    mm.then_inc(op_done, 1)

            def chunk(k, i, c):
                g = group(i, c)
                for r in range(4):
                    for t in range(4):
                        if within(k, CHUNKS):
                            scores_T(k, i, c, 4 * r + t)
                        if within(k + 3, CHUNKS):
                            scores(k, i, c, 4 * r + t)
                    if r == 0 and within(k - 1, CHUNKS):
                        values(k - 1, *ahead(i, c, -1), 3)
                    if r > 0 and within(k, CHUNKS):
                        values(k, i, c, r - 1)
                    if r == 0 and c % 2 == 1 and within(g - 1, GROUPS):
                        output(k, i, c)
                    if r == 2 and within(k + 2, CHUNKS):
                        if isinstance(k, int) and k == -2:
                            pe.wait_ge(consts_in, 32)
                            pe.wait_ge(consts_set, 6)
                            pe.wait_ge(blank_set, 3)
                        pe.wait_ge(negmax_set, k + 3)
                        need(pe, row_set, k + 2)
                        need(pe, acc_done3, 2 * (g - 2 + c % 2) + 1)
                        for t in range(CT):
                            mm = nc.tensor.transpose(m_bank[0][0:DH + 1, P * t:P * (t + 1)], neg_max[c % 2][:, t, :], ident[:, :])
                        mm.then_inc(row_done, 1)
                    if r == 1 and c % 2 == 0 and within(g - 1, GROUPS):
                        pe.wait_ge(add_done, sum(ADDS) * g)
                        need(pe, acc_done3, 2 * (g - 1))
                        for u in range(2):
                            mm = nc.tensor.matmul(m_bank[1][DH * u:DH * (u + 1), :], ones_sb[:, :], sums[(c // 2 - 1) % 2][:, u, :],
                                                  start=True, stop=True)
                        mm.then_inc(l_done, 1)

            rolled(pe, chunk)

        @block.scalar
        def _(act):
            def chunk(k, i, c):
                for n in range(ST):
                    if within(k, CHUNKS):
                        if n % 4 == 0:
                            need(act, pv_done, 4 * k + n // 4 - 1)
                        if n % 2 == 0 and (n >= 8 or not isinstance(k, int) or k > 0):
                            before, pair = (k, n // 2 - 4) if n >= 8 else (k - 1, n // 2 + 4)
                            if pair % 4 >= 2:
                                act.wait_ge(pair_done, 2 * before + pair // 4 + 1)
                            else:
                                act.wait_ge(add_done, adds(*(ahead(i, c, 0) if n >= 8 else ahead(i, c, -1)), pair))
                        act.wait_ge(s_done, 16 * k + n + 1)
                        nc.scalar.activation(probs[:, n % 8, :], s_bank[n % 2][:, :], ACT.Exp, scale=SCALE).then_inc(exp_done, 1)
                    if n == 11 and within(k + 2, CHUNKS):
                        q = CH * (ahead(i, c, 2)[1] // 2 % QC)
                        act.wait_ge(row_done, k + 3)
                        nc.scalar.activation(q_lm[c % 2][DH:DH + 1, q:q + CH], m_bank[0][DH:DH + 1, :], ACT.Copy).then_inc(row_set, 1)

            rolled(act, chunk)

        @block.vector
        def _(dve):
            for n in range(2):
                nc.vector.memset(neg_max[n][:, :, :], 0.0).then_inc(blank_set, 1)
            nc.vector.memset(ones_sb[:, :], 1.0).then_inc(blank_set, 1)
            dve.wait_ge(blank_set, 3)

            def add_output(k, i, c, half):
                g = group(i, c) - 1
                if isinstance(g, int) and g == 0:
                    dve.wait_ge(acc_in, 16)
                i1, c1 = ahead(i, c, -3)
                tile = TILES // B * (i1 // (PAIRS // B // 2)) + CT * (c1 // 2 % QC) + 2 * half
                at = acc[:, bass.ds(tile, 2), :]
                dve.wait_ge(op_done, 2 * g + half + 1)
                need(dve, acc_done3, 2 * g + half - 7)
                need(dve, mixed, g + 1)
                nc.vector.tensor_tensor(at, m_bank[half][:, :].rearrange("p (t n) -> p t n", n=D), at, ALU.add
                                        ).then_inc(acc_done3, 1)

            def add_pair(k, i, c, n):
                dve.wait_ge(exp_done, 16 * k + 8 * n + 8)
                if not isinstance(k, int) or k > 0:
                    dve.wait_ge(add_done, adds(*ahead(i, c, -1), 4 * n + 3))
                nc.vector.tensor_tensor(pair_sum[n][:, :, :], probs[:, 4:6, :], probs[:, 6:8, :], ALU.add).then_inc(pair_done, 1)

            def chunk(k, i, c):
                g = group(i, c)
                for r in range(4):
                    for n in range(4 * r, 4 * r + 4):
                        if within(k + 3, CHUNKS):
                            dve.wait_ge(a_done, 16 * (k + 3) + n + 1)
                            nc.vector.tensor_reduce(maxes[(c + 1) % 2][:, r, n % 4:n % 4 + 1], a_bank[n % 2][:, :], AX.X, ALU.max
                                                    ).then_inc(max_done[n % 2], 1)
                        if n == 1 and within(k - 1, CHUNKS):
                            add_pair(k - 1, *ahead(i, c, -1), 1)
                        if n == 9 and within(k, CHUNKS):
                            add_pair(k, i, c, 0)
                        if r == 1 and n % 2 == 1 and c % 2 == 1 and within(g - 1, GROUPS):
                            add_output(k, i, c, n % 4 // 2)
                        if r >= 2 and n % 2 == 1 and c % 2 == 0 and within(g - 1, GROUPS):
                            part = slice(P * ((n - 8) // 2), P * ((n - 8) // 2 + 1))
                            dve.wait_ge(l_done, g)
                            need(dve, norm_done, g - 1)
                            nc.vector.reciprocal(rsum[:, part], m_bank[1][:, part]).then_inc(rsum_set, 1)
                if c % 2 == 1 and within(k, CHUNKS):
                    n, tile = c // 2 % 2, 4 * i + c // 4
                    if isinstance(k, int) and k == 1:
                        dve.wait_ge(acc_in, 16)
                    dve.wait_ge(fetched[n], 16 * (tile + 1))
                    need(dve, acc_done3, 2 * g)
                    need(dve, mixed, g)
                    at = acc[:, bass.ds(tile, 1), :].rearrange("p t d -> p (t d)")
                    nc.vector.scalar_tensor_tensor(at, y_in[n][:, :], weights[:, n, bass.ds(tile, 1)], at, ALU.mult, ALU.add
                                                   ).then_inc(mixed, 1)
                if within(k + 3, CHUNKS):
                    for n in range(2):
                        dve.wait_ge(max_done[n], 8 * (k + 4))
                    need(dve, row_done, k + 2)
                    nc.vector.tensor_reduce(neg_max[(c + 1) % 2][:, :, DH:DH + 1], maxes[(c + 1) % 2][:, :, :], AX.X, ALU.max, negate=True
                                            ).then_inc(negmax_set, 1)
                if c % 2 == 0 and within(g - 1, GROUPS):
                    dve.wait_ge(rsum_set, 4 * g)
                    dve.wait_ge(pv_done, 4 * k)
                    need(dve, op_done, 2 * (g - 2))
                    v = (c // 2 - 1) % 2
                    nc.vector.tensor_tensor(normed[v][:, :], o_bank[v][:, :], rsum[:, :], ALU.mult).then_inc(norm_done, 1)

            rolled(dve, chunk)

        @block.gpsimd
        def _(pool):
            def chunk(k, i, c):
                if not within(k, CHUNKS):
                    return
                g = group(i, c)
                if c % 2 == 0:
                    n, tile = c // 2 % 2, 4 * i + c // 4
                    need(pool, mixed, g - 1)
                    need(pool, fetched[n], 16 * tile)
                    nc.gpsimd.tensor_copy(slot_now[n][:, :], slots[:, n, bass.ds(tile, 1)]).then_inc(slot_set, 1)
                    pool.wait_ge(slot_set, g + 1)
                    pool.sem_inc(passed3, 1)
                    nc.gpsimd.indirect_dma_start(y_in[n][:, :], None, y_rows, bass.IndirectOffsetOnAxis(ap=slot_now[n][:, :], axis=0)
                                                 ).then_inc(fetched[n], 16)
                    need(pool, l_done, g - 1)
                total = sums[c // 2 % 2]
                for pair in ((1, 3, 4, 5, 7) if c % 2 == 0 else (0, 1, 3, 4, 5, 7)):
                    if pair % 4 == 3:
                        pool.wait_ge(pair_done, 2 * k + pair // 4 + 1)
                        term = pair_sum[pair // 4][:, :, :]
                    else:
                        pool.wait_ge(exp_done, 16 * k + 2 * pair + 2)
                        term = probs[:, 2 * (pair % 4):2 * (pair % 4) + 2, :]
                    first = c % 2 == 0 and pair == 1
                    need(pool, add_done, adds(i, c, pair) - 1)
                    nc.gpsimd.tensor_tensor(total[:, :, :], probs[:, 0:2, :] if first else total[:, :, :], term, ALU.add
                                            ).then_inc(add_done, 1)

            for n in range(2):
                nc.gpsimd.memset(q_lm[n][DH:DH + 1, :].bitcast(F32), 0.0).then_inc(consts_set, 1)
                for w in range(2):
                    nc.gpsimd.memset(k_h1[w][n][DH:DH + 1, :].bitcast(F32), 1.0).then_inc(consts_set, 1)
            pool.wait_ge(consts_set, 6)
            rolled(pool, chunk)


def program(nc, x, wdq, wdkv, w_qk, wuv, w_out, ln_scale, ln_bias, router, w_gu, w_dn,
            identity, iota, earlier, iota_tiles, cos_t, sin_t, out):
    def scratch(name, shape):
        return nc.dram_tensor(name, shape, F32).ap()

    v_scratch = scratch("v_scratch", (TOKENS // CH, P, H, CT, DH))
    qk_scratch = scratch("qk_scratch", (PAIRS, P, 4, S))
    xn_scratch = scratch("xn_scratch", (TOKENS // CH, CH, D))
    acc_scratch = scratch("acc_scratch", (P, TILES, D))
    slot_rows = scratch("slot_rows", (SLOT_TILES * P, D))
    y_rows = scratch("y_rows", (SLOT_TILES * P, D))
    with ExitStack() as ctx:
        slots = ctx.enter_context(nc.sbuf_tensor("slots", [P, CHOICES, TILES], U32))
        weights = ctx.enter_context(nc.sbuf_tensor("weights", [P, CHOICES, TILES], F32))
        with ExitStack() as inner:
            cT = inner.enter_context(nc.sbuf_tensor("cT", [P, 2, TOKENS], F32))
            tile_expert = inner.enter_context(nc.sbuf_tensor("tile_expert", [1, SLOT_TILES], mybir.dt.int32))
            phase_norm(nc, x, wdq, wdkv, wuv, router, ln_scale, ln_bias, identity, iota, earlier, iota_tiles,
                       v_scratch, xn_scratch, acc_scratch, slot_rows, cT, slots, weights, tile_expert)
            phase_experts(nc, w_gu, w_dn, w_qk, cos_t, sin_t, identity, xn_scratch, slot_rows, y_rows, qk_scratch,
                          cT, slots, tile_expert)
        phase_attention(nc, identity, w_out, qk_scratch, v_scratch, acc_scratch, y_rows, slots, weights, out)


def rotary_tables():
    inv_freq = 1.0 / 10000.0 ** (np.arange(0, DH, 2, dtype=np.float32) / DH)
    freqs = np.outer(np.arange(S, dtype=np.float32), inv_freq)
    cos = np.concatenate([np.cos(freqs), np.cos(freqs)], -1)[:, ::2]
    sin = np.concatenate([np.sin(freqs), np.sin(freqs)], -1)[:, ::2]
    c, s = cos.T.astype(np.float32), sin.T.astype(np.float32)
    return np.concatenate([c, c, c, c]), np.concatenate([-s, s, -s, s])


def kernel(**inputs):
    import concourse.bacc as _bacc
    from concourse.bass_utils import run_bass_kernel_spmd as _run

    a = {n.removeprefix("L0_"): np.asarray(v) for n, v in inputs.items()}

    def rows_of_heads(w, flip):
        r = w.reshape(H // 2, 2, DH // 2, 2, LATENT)
        r = r[:, :, :, ::-1] if flip else r
        return r.transpose(0, 4, 1, 3, 2).reshape(H // 2, LATENT, P)

    up_q, up_k = a["attn_w_up_q"], a["attn_w_up_k"]
    cos_t, sin_t = rotary_tables()
    arrays = {
        "x": a["attn_x"].reshape(TOKENS, D),
        "wdq": a["attn_w_down_q"].T,
        "wdkv": a["attn_w_down_kv"].T,
        "w_qk": np.stack([rows_of_heads(w, f) for w in (up_q, up_k) for f in (False, True)], axis=2),
        "wuv": a["attn_w_up_v"].T,
        "w_out": a["attn_w_out"].T,
        "ln_scale": a["attn_ln_scale"].reshape(KD, P).T,
        "ln_bias": a["attn_ln_bias"].reshape(KD, P).T,
        "router": a["ffn_router_w"],
        "w_gu": a["ffn_w_gate_up"].reshape(E, KD, P, 2 * F).transpose(2, 0, 1, 3),
        "w_dn": a["ffn_w_down"].reshape(E, F // P, P, D).transpose(2, 0, 1, 3),
        "identity": np.eye(P, dtype=np.float32),
        "iota": np.tile(np.arange(E, dtype=np.float32), (P, 1)),
        "earlier": np.triu(np.ones((P, P), np.float32), 1),
        "iota_tiles": np.repeat(np.arange(SLOT_TILES, dtype=np.float32), E)[None],
        "cos_t": cos_t,
        "sin_t": sin_t,
    }
    nc = _bacc.Bacc("TRN2", target_bir_lowering=False, num_devices=1)
    feeds, args = {}, []
    for name, array in arrays.items():
        feeds[f"in_{name}"] = np.ascontiguousarray(array)
        args.append(nc.dram_tensor(f"in_{name}", array.shape, F32, kind="ExternalInput").ap())
    args.append(nc.dram_tensor("out_0", (TOKENS, D), F32, kind="ExternalOutput").ap())
    program(nc, *args)
    r = _run(nc, [feeds], core_ids=[0])
    return r.results[0]["out_0"].reshape(B, S, D)
```

```python
from contextlib import ExitStack

import concourse.bass as bass
import numpy as np
from concourse import mybir

ALU = mybir.AluOpType
ACT = mybir.ActivationFunctionType
AX = mybir.AxisListType
F32 = mybir.dt.float32
F32R = mybir.dt.float32r
U32 = mybir.dt.uint32

P = 128
B, S, D = 2, 2048, 256
H, DH = 16, 64
E, F = 16, 256
LATENT = 128
TOKENS = B * S
TILES = TOKENS // P
CH = 512
CT = CH // P
KD = D // P
KT = S // P
QC = S // CH
EPS = 1e-5
SCALE = 1.0 / 8.0
PAIRS = B * H // 2
CHOICES = 2
SLOT_TILES = 80
assert SLOT_TILES >= CHOICES * TOKENS // P + E - 1


def need(eng, semaphore, value):
    if isinstance(value, int) and value <= 0:
        return
    eng.wait_ge(semaphore, value)


def within(n, total):
    return not isinstance(n, int) or 0 <= n < total


class Memory:

    def __init__(self, nc, ctx):
        self.nc, self.ctx = nc, ctx

    def sb(self, name, shape, dtype=F32):
        return self.ctx.enter_context(self.nc.sbuf_tensor(name, shape, dtype))

    def bank(self, name):
        return self.ctx.enter_context(self.nc.psum_tensor(name, [P, CH], F32))

    def sem(self, name):
        return self.ctx.enter_context(self.nc.semaphore(name))


def phase_norm(nc, x, wdq, wdkv, wuv, router, ln_scale, ln_bias, identity, iota, earlier, iota_tiles,
               v_scratch, xn_scratch, acc_scratch, slot_rows, cT, slots, weights, tile_expert):
    chunks = TOKENS // CH
    with ExitStack() as ctx:
        m = Memory(nc, ctx)
        x_in = [m.sb(f"x_in{u}", [P, CT, D]) for u in range(2)]
        xn = [m.sb(f"xn{u}", [P, CT, D]) for u in range(2)]
        xn2 = [m.sb(f"xn2_{u}", [P, CT, D]) for u in range(2)]
        stats = m.sb("stats", [P, 2, CT, 6])
        moments = m.sb("moments", [P, 2, CT, 2])
        var_eps = m.sb("var_eps", [P, 2, CT])
        minus_half = m.sb("minus_half", [P, CT])
        rstd = m.sb("rstd", [P, 2, CT])
        xnT_c = [m.sb(f"xnT_c{u}", [P, KD, CH]) for u in range(2)]
        hT_c = [m.sb(f"hT_c{u}", [P, KD, CH]) for u in range(2)]
        c_c = [m.sb(f"c_c{u}", [P, 2, CH]) for u in range(2)]
        v_c = [m.sb(f"v_c{u}", [P, H, CT, DH]) for u in range(2)]
        logits = m.sb("logits", [P, CT, E])
        wdq_sb = m.sb("wdq_sb", [P, KD, LATENT])
        wdkv_sb = m.sb("wdkv_sb", [P, KD, LATENT])
        wuv_sb = m.sb("wuv_sb", [P, H * DH])
        router_sb = m.sb("router_sb", [P, KD, E])
        res_c = [m.sb(f"res_c{u}", [P, CT, D]) for u in range(2)]
        EMPTY = SLOT_TILES // chunks
        zeros = m.sb("zeros", [P, EMPTY * D])
        earlier_sb = m.sb("earlier_sb", [P, P])
        all_ones = m.sb("all_ones", [P, P])
        iota_tiles_sb = m.sb("iota_tiles_sb", [1, SLOT_TILES * E])
        scale_sb = m.sb("scale_sb", [P, KD])
        bias_sb = m.sb("bias_sb", [P, KD])
        ident = m.sb("ident", [P, P])
        iota_sb = m.sb("iota_sb", [P, E])
        top = m.sb("top", [P, CT, 8])
        top_at = m.sb("top_at", [P, CT, 8], U32)
        top_atf = m.sb("top_atf", [P, CT, 2])
        gap = m.sb("gap", [P, TILES])
        ratio = m.sb("ratio", [P, TILES])
        denom = m.sb("denom", [P, TILES])
        chosen = [m.sb(f"chosen{n}", [P, TILES, E]) for n in range(CHOICES)]
        both = m.sb("both", [P, TILES, E])
        totals = m.sb("totals", [P, TILES, E])
        upto = [m.sb(f"upto{n}", [P, TILES, E]) for n in range(2)]
        picked = [m.sb(f"picked{n}", [P, TILES, E]) for n in range(CHOICES)]
        slots_f = m.sb("slots_f", [P, CHOICES, TILES])
        tiles_i = m.sb("tiles_i", [P, E], mybir.dt.int32)
        tiles_f = m.sb("tiles_f", [P, E])
        ends = [m.sb(f"ends{n}", [P, E]) for n in range(2)]
        starts = m.sb("starts", [P, E])
        past = m.sb("past", [1, SLOT_TILES, E])
        expert_f = m.sb("expert_f", [1, SLOT_TILES])
        t_bank = [m.bank(f"t_bank{n}") for n in range(4)]
        c_bank = [m.bank(f"c_bank{n}") for n in range(2)]
        v_bank = [m.bank(f"v_bank{n}") for n in range(2)]

        weights_in = m.sem("weights_in")
        x_loaded = [m.sem(f"x_loaded{u}") for u in range(2)]
        norm1 = m.sem("norm1")
        norm2 = m.sem("norm2")
        small = m.sem("small")
        half_set = m.sem("half_set")
        passed = m.sem("passed")
        rstd_set = m.sem("rstd_set")
        turned = m.sem("turned")
        evac_x = m.sem("evac_x")
        evac_h = m.sem("evac_h")
        latent = m.sem("latent")
        latent_out = m.sem("latent_out")
        v_done = m.sem("v_done")
        v_out = m.sem("v_out")
        routed = m.sem("routed")
        routed_out = m.sem("routed_out")
        acc_set = m.sem("acc_set")
        kept_x = [m.sem(f"kept_x{u}") for u in range(2)]
        kept_r = [m.sem(f"kept_r{u}") for u in range(2)]
        kept_v = [m.sem(f"kept_v{u}") for u in range(2)]
        gap_set = m.sem("gap_set")
        ratio_set = m.sem("ratio_set")
        picked_set = m.sem("picked_set")
        route = m.sem("route")
        counted = m.sem("counted")
        zeros_set = m.sem("zeros_set")
        cleared = m.sem("cleared")

        block = ctx.enter_context(nc.Block())
        x_t = x.rearrange("(m j p) d -> m p j d", p=P, j=CT)
        PICKS = 6
        VN = 2 * CT

        def rolled(eng, step):
            for n in range(4):
                step(n // 2, n % 2)
            with eng.Fori(2, chunks // 2) as i:
                for u in range(2):
                    step(i, u)
            step(chunks // 2, 0)

        def previous(i, u):
            return (i, 0) if u == 1 else (i - 1, 1)

        @block.sync
        def _(sp):
            def load(i, u):
                sp.dma_start(x_in[u][:, :, :], x_t[2 * i + u]).then_inc(x_loaded[u], 16)

            load(0, 0)
            load(0, 1)
            sp.dma_start(ident[:, :], identity).then_inc(weights_in, 16)
            sp.dma_start(scale_sb[:, :], ln_scale).then_inc(weights_in, 16)
            sp.dma_start(bias_sb[:, :], ln_bias).then_inc(weights_in, 16)
            sp.dma_start(wdq_sb[:, :, :], wdq.rearrange("(k p) c -> p k c", p=P)).then_inc(weights_in, 16)
            sp.dma_start(wdkv_sb[:, :, :], wdkv.rearrange("(k p) c -> p k c", p=P)).then_inc(weights_in, 16)
            sp.dma_start(wuv_sb[:, :], wuv).then_inc(weights_in, 16)
            sp.dma_start(router_sb[:, :, :], router.rearrange("(k p) e -> p k e", p=P)).then_inc(weights_in, 16)
            sp.dma_start(iota_sb[:, :], iota).then_inc(weights_in, 16)
            sp.dma_start(earlier_sb[:, :], earlier).then_inc(weights_in, 16)
            sp.dma_start(iota_tiles_sb[:, :], iota_tiles).then_inc(weights_in, 16)

            def norms(i, u, more):
                n = 2 * i + u
                sp.wait_ge(norm1, CT * (n + 1))
                sp.sem_inc(passed, 1)
                sp.dma_start(xn_scratch[n].rearrange("(j p) d -> p j d", p=P), xn[u][:, :, :]).then_inc(kept_x[u], 16)
                sp.wait_ge(acc_set, n + 1)
                sp.sem_inc(passed, 1)
                sp.dma_start(acc_scratch[:, bass.ds(CT * n, CT), :], res_c[u][:, :, :]).then_inc(kept_r[u], 16)
                if more:
                    load(i + 1, u)

            def products(i, u):
                n = 2 * i + u
                sp.wait_ge(latent_out, 2 * (n + 1))
                sp.sem_inc(passed, 1)
                sp.dma_start(cT[:, :, bass.ds(CH * n, CH)], c_c[u][:, :, :]).then_inc(kept_v[u], 16)
                sp.wait_ge(v_out, VN * (n + 1))
                sp.sem_inc(passed, 1)
                sp.dma_start(v_scratch[n], v_c[u][:, :, :, :]).then_inc(kept_v[u], 16)

            norms(0, 0, True)
            norms(0, 1, True)
            products(0, 0)
            with sp.Fori(1, chunks // 2 - 1) as i:
                for u in range(2):
                    norms(i, u, True)
                    products(*previous(i, u))
            for u in range(2):
                norms(chunks // 2 - 1, u, False)
                products(*previous(chunks // 2 - 1, u))
            products(chunks // 2 - 1, 1)
            for u in range(2):
                sp.wait_ge(kept_x[u], 16 * (chunks // 2))
                sp.wait_ge(kept_r[u], 16 * (chunks // 2))
                sp.wait_ge(kept_v[u], 32 * (chunks // 2))

        @block.vector
        def _(dve):
            STEPS = 2 * (2 * CT + 1)

            def pick(n):
                def wait(semaphore, value):
                    dve.wait_ge(semaphore, value)
                    dve.sem_inc(passed, 1)
                tiles = bass.ds(CT * (n - 1), CT)
                base = PICKS * (n - 1)
                wait(routed_out, n)
                for j in range(CT):
                    ins = nc.vector.max(top[:, j, :], logits[:, j, :])
                ins.then_inc(picked_set, 1)
                wait(picked_set, base + 1)
                for j in range(CT):
                    ins = nc.vector.max_index(top_at[:, j, :], top[:, j, :], logits[:, j, :])
                nc.vector.tensor_tensor(gap[:, tiles], top[:, :, 1], top[:, :, 0], ALU.subtract).then_inc(gap_set, 1)
                ins.then_inc(picked_set, 1)
                wait(picked_set, base + 2)
                nc.vector.tensor_copy(top_atf[:, :, :], top_at[:, :, 0:CHOICES]).then_inc(picked_set, 1)
                wait(picked_set, base + 3)
                for choice in range(CHOICES):
                    nc.vector.tensor_tensor(chosen[choice][:, tiles, :], iota_sb[:, :].unsqueeze(1).broadcast_to([P, CT, E]),
                                            top_atf[:, :, choice:choice + 1].broadcast_to([P, CT, E]), ALU.is_equal
                                            ).then_inc(picked_set, 1)
                wait(picked_set, base + 5)
                nc.vector.tensor_tensor(both[:, tiles, :], chosen[0][:, tiles, :], chosen[1][:, tiles, :], ALU.add
                                        ).then_inc(picked_set, 1)

            def norm(i, u, which, src, dst, done):
                n = 2 * i + u
                base = STEPS * n + which * (2 * CT + 1)
                for j in range(CT):
                    nc.vector.bn_stats(stats[:, which, j, :], src[:, j, :]).then_inc(small, 1)
                dve.wait_ge(small, base + CT)
                dve.sem_inc(passed, 1)
                for j in range(CT):
                    nc.vector.bn_aggr(moments[:, which, j, :], stats[:, which, j, :]).then_inc(small, 1)
                dve.wait_ge(small, base + 2 * CT)
                nc.vector.tensor_scalar(var_eps[:, which, :], moments[:, which, :, 1], EPS, None,
                                        ALU.add).then_inc(small, 1)
                if which == 0 and within(n - 2, chunks):
                    pick(n - 1)
                dve.wait_ge(rstd_set, 2 * n + which + 1)
                for j in range(CT):
                    nc.vector.tensor_scalar(dst[:, j, :], src[:, j, :], moments[:, which, j, 0:1],
                                            rstd[:, which, j:j + 1], ALU.subtract, ALU.mult).then_inc(done, 1)

            def step(i, u):
                n = 2 * i + u
                if within(n, chunks):
                    dve.wait_ge(x_loaded[u], 16 * (i + 1))
                    need(dve, turned, 4 * (n - 1))
                    need(dve, acc_set, n - 1)
                    need(dve, kept_x[u], 16 * i)
                    norm(i, u, 0, x_in[u], xn[u], norm1)
                    dve.wait_ge(norm1, CT * (n + 1))
                    norm(i, u, 1, xn[u], xn2[u], norm2)
                    if isinstance(n, int) and n == 0:
                        dve.wait_ge(weights_in, 16 * 10)
                    need(dve, latent, 2 * (n - 1))
                    for k in range(KD):
                        dve.wait_ge(turned, 4 * n + 3 + k)
                        nc.vector.tensor_scalar(hT_c[u][:, k, :], t_bank[2 + k][:, :], scale_sb[:, k:k + 1],
                                                bias_sb[:, k:k + 1], ALU.mult, ALU.add).then_inc(evac_h, 1)
                if within(n - 1, chunks):
                    dve.wait_ge(routed, n)
                    if not within(n, chunks):
                        pick(n - 1)
                    nc.vector.tensor_copy(logits[:, :, :],
                                          c_bank[0][:, 0:CT * E].rearrange("p (j e) -> p j e", e=E)).then_inc(routed_out, 1)
                    if not within(n, chunks):
                        pick(n)

            rolled(dve, step)

            step = [0]

            def link(ins):
                step[0] += 1
                ins.then_inc(route, 1)
                dve.wait_ge(route, step[0])

            dve.wait_ge(picked_set, PICKS * chunks)

            full = [P, TILES, E]
            dve.wait_ge(counted, 2)
            flat = "p (t e) -> p t e"
            link(nc.vector.tensor_copy(totals[:, :, :], t_bank[1][:, :].rearrange(flat, e=E)))
            source, at, by = totals, 0, 1
            while by < TILES:
                link(nc.vector.tensor_copy(upto[at][:, 0:by, :], source[:, 0:by, :]))
                link(nc.vector.tensor_tensor(upto[at][:, by:, :], source[:, by:, :], source[:, 0:TILES - by, :], ALU.add))
                source, at, by = upto[at], 1 - at, 2 * by
            count = source[:, TILES - 1, :]
            link(nc.vector.tensor_scalar(tiles_f[:, :], count, float(P - 1), None, ALU.add))
            link(nc.vector.tensor_copy(tiles_i[:, :], tiles_f[:, :]))
            link(nc.vector.tensor_scalar(tiles_i[:, :], tiles_i[:, :], 7, None, ALU.logical_shift_right))
            link(nc.vector.tensor_copy(tiles_f[:, :], tiles_i[:, :]))
            end, to, by = tiles_f, 0, 1
            while by < E:
                link(nc.vector.tensor_copy(ends[to][:, 0:by], end[:, 0:by]))
                link(nc.vector.tensor_tensor(ends[to][:, by:], end[:, by:], end[:, 0:E - by], ALU.add))
                end, to, by = ends[to], 1 - to, 2 * by
            link(nc.vector.tensor_tensor(starts[:, :], end[:, :], tiles_f[:, :], ALU.subtract))
            link(nc.vector.tensor_scalar(starts[:, :], starts[:, :], float(P), None, ALU.mult))

            link(nc.vector.tensor_tensor(source[:, :, :], source[:, :, :], totals[:, :, :], ALU.subtract))
            link(nc.vector.tensor_tensor(source[:, :, :], t_bank[0][:, :].rearrange(flat, e=E), source[:, :, :], ALU.add))
            link(nc.vector.tensor_tensor(source[:, :, :], source[:, :, :], starts[:, :].unsqueeze(1).broadcast_to(full), ALU.add))
            for n in range(CHOICES):
                link(nc.vector.tensor_tensor(picked[n][:, :, :], source[:, :, :], chosen[n][:, :, :], ALU.mult))
                link(nc.vector.tensor_reduce(slots_f[:, n, :], picked[n][:, :, :], AX.X, ALU.add))
            link(nc.vector.tensor_copy(slots[:, :, :], slots_f[:, :, :]))

            tiles_by_e = [1, SLOT_TILES, E]
            link(nc.vector.tensor_tensor(past[:, :, :], iota_tiles_sb[:, :].rearrange(flat, e=E),
                                         end[0:1, :].unsqueeze(1).broadcast_to(tiles_by_e), ALU.is_ge))
            link(nc.vector.tensor_reduce(expert_f[:, :], past[:, :, :], AX.X, ALU.add))
            link(nc.vector.tensor_scalar(expert_f[:, :], expert_f[:, :], float(E - 1), None, ALU.min))
            link(nc.vector.tensor_copy(tile_expert[:, :], expert_f[:, :]))

            dve.wait_ge(ratio_set, 1)
            link(nc.vector.tensor_scalar(denom[:, :], ratio[:, :], 1.0, None, ALU.add))
            link(nc.vector.reciprocal(weights[:, 0, :], denom[:, :]))
            link(nc.vector.tensor_tensor(weights[:, 1, :], weights[:, 0, :], ratio[:, :], ALU.mult))

        @block.scalar
        def _(act):
            def step(i, u):
                n = 2 * i + u
                if within(n - 1, chunks):
                    i1, v = previous(i, u)
                    need(act, kept_v[v], 32 * i1)
                    need(act, v_done, VN * (n - 2))
                    for k in range(2):
                        act.wait_ge(latent, 2 * (n - 1) + 1 + k)
                        nc.scalar.activation(c_c[v][:, k, :], c_bank[k][:, :], ACT.Copy).then_inc(latent_out, 1)
                if within(n, chunks):
                    need(act, routed, n - 1)
                    for k in range(KD):
                        act.wait_ge(turned, 4 * n + 1 + k)
                        nc.scalar.activation(xnT_c[u][:, k, :], t_bank[k][:, :], ACT.Copy).then_inc(evac_x, 1)
                    act.dma_start(slot_rows.rearrange("(m p t) d -> m p (t d)", p=P, t=EMPTY)[n], zeros[:, :]).then_inc(cleared, 16)
                if within(n - 1, chunks):
                    for j in range(CT):
                        for half in range(2):
                            act.wait_ge(v_done, VN * (n - 1) + 2 * j + half + 1)
                            nc.scalar.activation(v_c[v][:, H // 2 * half:H // 2 * (half + 1), j, :],
                                                 v_bank[half][:, :].rearrange("p (h d) -> p h d", d=DH), ACT.Copy).then_inc(v_out, 1)

            act.wait_ge(zeros_set, 1)
            rolled(act, step)
            act.wait_ge(gap_set, chunks)
            nc.scalar.activation(ratio[:, :], gap[:, :], ACT.Exp).then_inc(ratio_set, 1)
            act.wait_ge(cleared, 16 * chunks)

        @block.gpsimd
        def _(pool):
            def step(i, u):
                n = 2 * i + u
                if not within(n, chunks):
                    return
                for which in range(2):
                    pool.wait_ge(small, (4 * CT + 2) * n + (which + 1) * (2 * CT + 1))
                    nc.gpsimd.tensor_tensor(rstd[:, which, :], var_eps[:, which, :], minus_half[:, :], ALU.pow
                                            ).then_inc(rstd_set, 1)
                pool.wait_ge(norm1, CT * (n + 1))
                need(pool, kept_r[u], 16 * i)
                nc.gpsimd.tensor_tensor(res_c[u][:, :, :], x_in[u][:, :, :], xn[u][:, :, :],
                                        ALU.add).then_inc(acc_set, 1)

            nc.gpsimd.memset(minus_half[:, :], -0.5).then_inc(half_set, 1)
            nc.gpsimd.memset(all_ones[:, :], 1.0).then_inc(half_set, 1)
            nc.gpsimd.memset(zeros[:, :], 0.0).then_inc(zeros_set, 1)
            pool.wait_ge(half_set, 2)
            rolled(pool, step)

        @block.tensor
        def _(pe):
            pe.wait_ge(weights_in, 16 * 10)

            def router_logits(n, v):
                need(pe, routed_out, n - 1)
                pe.wait_ge(evac_x, KD * n)
                for j in range(CT):
                    for k in range(KD):
                        mm = nc.tensor.matmul(c_bank[0][:, j * E:(j + 1) * E], xnT_c[v][:, k, j * P:(j + 1) * P],
                                              router_sb[:, k, :], start=(k == 0), stop=(k == KD - 1))
                mm.then_inc(routed, 1)

            def count_choices():
                pe.wait_ge(picked_set, PICKS * chunks)
                pe.wait_ge(evac_x, KD * chunks)
                for n, w in enumerate((earlier_sb, all_ones)):
                    nc.tensor.matmul(t_bank[n][:, :], w[:, :], both[:, :, :].rearrange("p t e -> p (t e)"), start=True, stop=True
                                     ).then_inc(counted, 1)

            def step(i, u):
                n = 2 * i + u
                _, v = previous(i, u)
                last = isinstance(n, int) and n == chunks
                if last:
                    pe.wait_ge(latent_out, 2 * (n - 1))
                    router_logits(n, v)
                    pe.wait_ge(half_set, 2)
                if within(n - 1, chunks):
                    need(pe, routed_out, n if last else n - 1)
                    pe.wait_ge(evac_h, KD * n)
                    for c, w in enumerate((wdq_sb, wdkv_sb)):
                        for k in range(KD):
                            mm = nc.tensor.matmul(c_bank[c][:, :], w[:, k, :], hT_c[v][:, k, :], start=(k == 0), stop=(k == KD - 1))
                        mm.then_inc(latent, 1)
                if within(n, chunks):
                    for which, (src, done, evac) in enumerate(((xn[u], norm1, evac_x), (xn2[u], norm2, evac_h))):
                        pe.wait_ge(done, CT * (n + 1))
                        for k in range(KD):
                            need(pe, evac, KD * (n - 1) + k + 1)
                            for j in range(CT):
                                mm = nc.tensor.transpose(t_bank[2 * which + k][:, j * P:(j + 1) * P],
                                                         src[:, j, k * P:(k + 1) * P], ident[:, :])
                            mm.then_inc(turned, 1)
                if within(n - 1, chunks):
                    pe.wait_ge(latent_out, 2 * n)
                    if last:
                        count_choices()
                    else:
                        router_logits(n, v)
                    for j in range(CT):
                        for half in range(2):
                            need(pe, v_out, VN * (n - 1) + 2 * (j - 1) + half + 1)
                            nc.tensor.matmul(v_bank[half][:, :], c_c[v][:, 1, j * P:(j + 1) * P],
                                             wuv_sb[:, half * CH:(half + 1) * CH], start=True, stop=True).then_inc(v_done, 1)

            rolled(pe, step)


def phase_experts(nc, w_gu, w_dn, w_qk, cos_t, sin_t, identity, xn_scratch, slot_rows, y_rows, qk_scratch,
                  cT, slots, tile_expert):
    PER = 16
    STEPS = PAIRS * 8
    FIRST = STEPS - SLOT_TILES
    assert FIRST == 3 * PER and SLOT_TILES % PER == 0 and E == PER
    with ExitStack() as ctx:
        m = Memory(nc, ctx)
        gu_sb = m.sb("gu_sb", [P, E, KD, 2 * F])
        dn_sb = m.sb("dn_sb", [P, E, F // P, D])
        qk_sb = [m.sb(f"qk_sb{u}", [P, 4, P]) for u in range(2)]
        ident = m.sb("ident2", [P, P])
        cos_sb = m.sb("cos_sb", [P, S])
        sin_sb = m.sb("sin_sb", [P, S])
        by_cos = [m.sb(f"by_cos{u}", [P, CH]) for u in range(2)]
        by_sin = [m.sb(f"by_sin{u}", [P, CH]) for u in range(2)]
        rot = [m.sb(f"rot{u}", [P, CH]) for u in range(2)]
        hi = [m.sb(f"hi{u}", [P, CH], F32R) for u in range(2)]
        lo = [m.sb(f"lo{u}", [P, CH], F32R) for u in range(2)]
        STAGES = 2
        stage = [m.sb(f"stage{n}", [P, CT, D]) for n in range(STAGES)]
        rows = [m.sb(f"rows{u}", [P, D]) for u in range(2)]
        rowsT = [m.sb(f"rowsT{u}", [P, KD, P]) for u in range(2)]
        silu = [m.sb(f"silu{u}", [P, F]) for u in range(2)]
        gated = [m.sb(f"gated{u}", [P, F]) for u in range(2)]
        gatedT = [m.sb(f"gatedT{u}", [P, F // P, P]) for u in range(2)]
        y = [m.sb(f"y{u}", [P, D]) for u in range(2)]
        pr_bank = [m.bank(f"pr_bank{n}") for n in range(2)]
        xt_bank = m.bank("xt_bank")
        gu_bank = [m.bank(f"gu_bank{n}") for n in range(2)]
        gt_bank = m.bank("gt_bank")
        y_bank = m.bank("y_bank")

        tables_in = m.sem("tables_in")
        experts_in = m.sem("experts_in")
        passed2 = m.sem("passed2")
        w_in = [m.sem(f"w_in{u}") for u in range(2)]
        pr_done = m.sem("pr_done")
        mul_done = m.sem("mul_done")
        rot_done = m.sem("rot_done")
        hi_done = m.sem("hi_done")
        lo_done = m.sem("lo_done")
        stored = [m.sem(f"stored{u}") for u in range(2)]
        staged = [m.sem(f"staged{n}") for n in range(STAGES)]
        scattered = [m.sem(f"scattered{n}") for n in range(STAGES)]
        rows_in = [m.sem(f"rows_in{u}") for u in range(2)]
        xt_done = m.sem("xt_done")
        xt_set = m.sem("xt_set")
        g_done = m.sem("g_done")
        silu_done = m.sem("silu_done")
        gated_set = m.sem("gated_set")
        gt_done = m.sem("gt_done")
        gt_set = m.sem("gt_set")
        y_done = m.sem("y_done")
        y_set = m.sem("y_set")
        y_kept = [m.sem(f"y_kept{u}") for u in range(2)]

        block = ctx.enter_context(nc.Block())

        def rolled(eng, step):
            def turn(i, tiles):
                for j in range(PER):
                    step(PER * i + j, i, j, tiles)
            turn(0, False)
            with eng.Fori(1, FIRST // PER) as i:
                turn(i, False)
            turn(FIRST // PER, True)
            with eng.Fori(FIRST // PER + 1, STEPS // PER - 1) as i:
                turn(i, True)
            turn(STEPS // PER - 1, True)
            for j in range(3):
                step(STEPS + j, STEPS // PER, j, True)

        def uses(i, j):
            return PER // 2 * i + j // 2 - FIRST // 2

        @block.sync
        def _(sp):
            def load_pair(pair, u):
                sp.dma_start(qk_sb[u][:, :, :], w_qk[pair % (H // 2)]).then_inc(w_in[u], 16)

            def load_rows(f, i, j):
                need(sp, xt_done, f - 1)
                sp.dma_start(rows[j % 2][:, :], slot_rows.rearrange("(t p) d -> t p d", p=P)[f]).then_inc(rows_in[j % 2], 16)

            load_pair(0, 0)
            sp.dma_start(cos_sb[:, :], cos_t).then_inc(tables_in, 16)
            sp.dma_start(sin_sb[:, :], sin_t).then_inc(tables_in, 16)
            sp.dma_start(ident[:, :], identity).then_inc(tables_in, 16)

            def step(s, i, j, tiles):
                u = j // 8 % 2
                f = s - FIRST
                if tiles and isinstance(f, int) and f == 0:
                    for n in range(STAGES):
                        sp.wait_ge(scattered[n], 16 * CHOICES * TILES // STAGES)
                    load_rows(0, i, j)
                    load_rows(1, i, j + 1)
                if within(s, STEPS):
                    if j % 8 == 2 and (not isinstance(i, int) or 2 * i + u + 1 < PAIRS):
                        need(sp, pr_done, 16 * (2 * i + u))
                        sp.sem_inc(passed2, 1)
                        load_pair(2 * i + u + 1, 1 - u)
                    at = slice(CH * (j % 4), CH * (j % 4 + 1))
                    sp.wait_ge(hi_done, s + 1)
                    sp.dma_start(qk_scratch[2 * i + u][:, 2 * (j % 8 // 4), at], hi[j % 2][:, :].bitcast(F32)).then_inc(stored[j % 2], 16)
                    sp.wait_ge(lo_done, s + 1)
                    sp.dma_start(qk_scratch[2 * i + u][:, 2 * (j % 8 // 4) + 1, at], lo[j % 2][:, :].bitcast(F32)).then_inc(stored[j % 2], 16)
                if tiles and within(f, SLOT_TILES) and within(f + 2, SLOT_TILES):
                    load_rows(f + 2, i, j)
                if tiles and within(f - 3, SLOT_TILES):
                    sp.wait_ge(y_set, f - 2)
                    sp.dma_start(y_rows.rearrange("(t p) d -> t p d", p=P)[f - 3], y[(j - 3) % 2][:, :]).then_inc(y_kept[(j - 3) % 2], 16)

            rolled(sp, step)
            for u in range(2):
                sp.wait_ge(stored[u], 32 * (STEPS // 2))
                sp.wait_ge(y_kept[u], 16 * (SLOT_TILES // 2))

        @block.tensor
        def _(pe):
            def step(s, i, j, tiles):
                u = j // 8 % 2
                f = s - FIRST
                if tiles and within(f - 1, SLOT_TILES):
                    gu_expert = pe.value_load(tile_expert[0:1, bass.ds(f - 1, 1)], min_val=0, max_val=E - 1)
                if tiles and within(f - 3, SLOT_TILES):
                    dn_expert = pe.value_load(tile_expert[0:1, bass.ds(f - 3, 1)], min_val=0, max_val=E - 1)
                if within(s, STEPS):
                    if j % 8 == 0:
                        pe.wait_ge(w_in[u], 16 * (i + 1))
                    sequence = (2 * i + u) // (H // 2)
                    for n in range(2):
                        need(pe, mul_done, 2 * (s - 1) + n + 1)
                        nc.tensor.matmul(pr_bank[n][:, :], qk_sb[u][:, 2 * (j % 8 // 4) + n, :],
                                         cT[:, j % 8 // 4, bass.ds(S * sequence + CH * (j % 4), CH)],
                                         start=True, stop=True).then_inc(pr_done, 1)
                if not tiles:
                    return
                if within(f, SLOT_TILES):
                    pe.wait_ge(tables_in, 48)
                    pe.wait_ge(rows_in[j % 2], 16 * (uses(i, j) + 1))
                    need(pe, xt_set, f)
                    for k in range(KD):
                        mm = nc.tensor.transpose(xt_bank[:, P * k:P * (k + 1)], rows[j % 2][:, P * k:P * (k + 1)], ident[:, :])
                    mm.then_inc(xt_done, 1)
                if within(f - 2, SLOT_TILES):
                    pe.wait_ge(gated_set, f - 1)
                    need(pe, gt_set, f - 2)
                    for k in range(F // P):
                        mm = nc.tensor.transpose(gt_bank[:, P * k:P * (k + 1)], gated[j % 2][:, P * k:P * (k + 1)], ident[:, :])
                    mm.then_inc(gt_done, 1)
                if within(f - 1, SLOT_TILES):
                    pe.wait_ge(experts_in, 32 * E)
                    pe.wait_ge(xt_set, f)
                    need(pe, gated_set, f - 2)
                    for k in range(KD):
                        mm = nc.tensor.matmul(gu_bank[(j - 1) % 2][:, :], rowsT[(j - 1) % 2][:, k, :],
                                              gu_sb[:, bass.ds(gu_expert, 1), k, :].rearrange("p e f -> p (e f)"),
                                              start=(k == 0), stop=(k == KD - 1))
                    mm.then_inc(g_done, 1)
                if within(f - 3, SLOT_TILES):
                    pe.wait_ge(gt_set, f - 2)
                    need(pe, y_set, f - 3)
                    for k in range(F // P):
                        mm = nc.tensor.matmul(y_bank[:, 0:D], gatedT[(j - 3) % 2][:, k, :],
                                              dn_sb[:, bass.ds(dn_expert, 1), k, :].rearrange("p e d -> p (e d)"),
                                              start=(k == 0), stop=(k == F // P - 1))
                    mm.then_inc(y_done, 1)

            rolled(pe, step)

        @block.scalar
        def _(act):
            act.wait_ge(tables_in, 48)
            act.wait_ge(w_in[0], 16)

            def step(s, i, j, tiles):
                f = s - FIRST
                if not tiles and (not isinstance(i, int) or i > 0) and j % 2 == 0:
                    e = PER // 2 * (i - 1) + j // 2
                    act.dma_start(gu_sb[:, bass.ds(e, 1), :, :], w_gu[:, bass.ds(e, 1), :, :]).then_inc(experts_in, 16)
                    act.dma_start(dn_sb[:, bass.ds(e, 1), :, :], w_dn[:, bass.ds(e, 1), :, :]).then_inc(experts_in, 16)
                if within(s - 1, STEPS):
                    v = (j - 1) % 2
                    act.wait_ge(rot_done, s)
                    need(act, lo_done, s - 2)
                    need(act, stored[v], 32 * (8 * i + (j - 1) // 2))
                    nc.scalar.activation(hi[v][:, :], rot[v][:, :], ACT.Copy).then_inc(hi_done, 1)
                if tiles and within(f - 2, SLOT_TILES):
                    act.wait_ge(gt_done, f - 1)
                    need(act, y_done, f - 3)
                    nc.scalar.activation(gatedT[j % 2][:, :, :], gt_bank[:, 0:F].rearrange("p (k t) -> p k t", t=P), ACT.Copy).then_inc(gt_set, 1)
                if tiles and within(f - 1, SLOT_TILES):
                    act.wait_ge(g_done, f)
                    need(act, gated_set, f - 2)
                    nc.scalar.activation(silu[(j - 1) % 2][:, :], gu_bank[(j - 1) % 2][:, 0:F], ACT.Silu).then_inc(silu_done, 1)

            rolled(act, step)

        @block.vector
        def _(dve):
            dve.wait_ge(tables_in, 48)

            def step(s, i, j, tiles):
                f = s - FIRST
                if within(s, STEPS):
                    need(dve, rot_done, s - 1)
                    at = slice(CH * (j % 4), CH * (j % 4 + 1))
                    for n, (out, table) in enumerate(((by_cos[j % 2], cos_sb), (by_sin[j % 2], sin_sb))):
                        dve.wait_ge(pr_done, 2 * s + n + 1)
                        nc.vector.tensor_tensor(out[:, :], pr_bank[n][:, :], table[:, at], ALU.mult).then_inc(mul_done, 1)
                if within(s - 1, STEPS):
                    v = (j - 1) % 2
                    dve.wait_ge(hi_done, s)
                    need(dve, stored[v], 32 * (8 * i + (j - 1) // 2))
                    nc.vector.tensor_tensor(lo[v][:, :], rot[v][:, :], hi[v][:, :], ALU.subtract).then_inc(lo_done, 1)
                if tiles and within(f, SLOT_TILES):
                    dve.wait_ge(xt_done, f + 1)
                    need(dve, g_done, f - 1)
                    nc.vector.tensor_copy(rowsT[j % 2][:, :, :], xt_bank[:, 0:D].rearrange("p (k t) -> p k t", t=P)).then_inc(xt_set, 1)
                if within(s, STEPS):
                    dve.wait_ge(mul_done, 2 * (s + 1))
                    need(dve, lo_done, s - 1)
                    need(dve, hi_done, s - 1)
                    nc.vector.tensor_tensor(rot[j % 2][:, :], by_cos[j % 2][:, :], by_sin[j % 2][:, :], ALU.add).then_inc(rot_done, 1)
                if tiles and within(f - 1, SLOT_TILES):
                    dve.wait_ge(silu_done, f)
                    need(dve, gt_done, f - 2)
                    nc.vector.tensor_tensor(gated[(j - 1) % 2][:, :], silu[(j - 1) % 2][:, :], gu_bank[(j - 1) % 2][:, F:2 * F], ALU.mult
                                            ).then_inc(gated_set, 1)
                if tiles and within(f - 3, SLOT_TILES):
                    dve.wait_ge(y_done, f - 2)
                    need(dve, y_kept[(j - 3) % 2], 16 * uses(i, j - 3))
                    nc.vector.tensor_copy(y[(j - 3) % 2][:, :], y_bank[:, 0:D]).then_inc(y_set, 1)

            rolled(dve, step)

        @block.gpsimd
        def _(pool):
            def scatter(n):
                u = n % STAGES
                pool.wait_ge(staged[u], 16 * (n // STAGES + 1))
                for t in range(CT):
                    for choice in range(CHOICES):
                        at = CT * n + t
                        nc.gpsimd.indirect_dma_start(slot_rows, bass.IndirectOffsetOnAxis(ap=slots[:, choice, at:at + 1], axis=0),
                                                     stage[u][:, t, :], None).then_inc(scattered[u], 16)

            for n in range(TILES // CT):
                u = n % STAGES
                if n >= STAGES:
                    pool.wait_ge(scattered[u], 16 * CHOICES * CT * (n // STAGES))
                pool.dma_start(stage[u][:, :, :], xn_scratch[n].rearrange("(j p) d -> p j d", p=P)).then_inc(staged[u], 16)
                if n > 0:
                    scatter(n - 1)
            scatter(TILES // CT - 1)

def phase_attention(nc, identity, row_mask, w_out, qk_scratch, v_scratch, acc_scratch, y_rows, slots, weights, out):
    CHUNKS = PAIRS * 8
    GROUPS = CHUNKS // 2
    PER = 16
    ST = 16
    KM = DH + CT
    Q_LOAD, K_LOAD, V_LOAD = 6 * 16, 4 * 16, 10 * 16
    ADDS = (6, 7)
    AFTER = ({0: 1, 1: 1, 3: 2, 4: 3, 5: 4, 6: 5, 7: 6}, {0: 1, 1: 2, 3: 3, 4: 4, 5: 5, 6: 6, 7: 7})
    with ExitStack() as ctx:
        m = Memory(nc, ctx)
        q_hh = [m.sb(f"q_hh{u}", [P, S], F32R) for u in range(2)]
        q_lm = [m.sb(f"q_lm{u}", [KM, S], F32R) for u in range(2)]
        k_hl = [[m.sb(f"k_hl{w}{u}", [P, S], F32R) for u in range(2)] for w in range(2)]
        k_h1 = [[m.sb(f"k_h1{w}{u}", [KM, S], F32R) for u in range(2)] for w in range(2)]
        v_sb = [[m.sb(f"v_sb{w}{u}", [P, KT, DH]) for u in range(2)] for w in range(2)]
        acc = m.sb("acc", [P, TILES, D])
        slot_now = [m.sb(f"slot_now{n}", [P, 1], U32) for n in range(CHOICES)]
        y_in = [m.sb(f"y_in{n}", [P, D]) for n in range(CHOICES)]
        w_out_sb = m.sb("w_out_sb", [P, H // 2, D])
        probs = m.sb("probs", [P, 8, CH])
        pair_sum = m.sb("pair_sum", [P, 2, CH])
        sums = [m.sb(f"sums{n}", [P, 2, CH]) for n in range(2)]
        rsum = m.sb("rsum", [P, CH])
        normed = [m.sb(f"normed{n}", [P, CH]) for n in range(2)]
        maxes = [m.sb(f"maxes{n}", [P, CT, 4]) for n in range(2)]
        neg_max = [m.sb(f"neg_max{n}", [P, KM]) for n in range(2)]
        ident = m.sb("ident3", [P, P])
        mask_sb = m.sb("mask_sb", [KM, CT, P])
        ones_sb = m.sb("ones_sb", [P, DH])
        s_bank = [m.bank(f"s_bank{n}") for n in range(2)]
        a_bank = [m.bank(f"a_bank{n}") for n in range(2)]
        o_bank = [m.bank(f"o_bank{n}") for n in range(2)]
        m_bank = [m.bank(f"m_bank{n}") for n in range(2)]

        consts_in = m.sem("consts_in")
        consts_set = m.sem("consts_set")
        blank_set = m.sem("blank_set")
        q_in = [m.sem(f"q_in{n}") for n in range(QC)]
        k_in = [m.sem(f"k_in{w}") for w in range(2)]
        v_in = [m.sem(f"v_in{w}") for w in range(2)]
        s_done = m.sem("s_done")
        exp_done = m.sem("exp_done")
        a_done = m.sem("a_done")
        max_done = [m.sem(f"max_done{n}") for n in range(2)]
        negmax_set = m.sem("negmax_set")
        row_done = m.sem("row_done")
        row_set = m.sem("row_set")
        pv_done = m.sem("pv_done")
        pair_done = m.sem("pair_done")
        add_done = m.sem("add_done")
        l_done = m.sem("l_done")
        rsum_set = m.sem("rsum_set")
        norm_done = m.sem("norm_done")
        op_done = m.sem("op_done")
        acc_done3 = m.sem("acc_done3")
        out_done = m.sem("out_done")
        acc_in = m.sem("acc_in")
        slot_set = m.sem("slot_set")
        fetched = [m.sem(f"fetched{n}") for n in range(CHOICES)]
        passed3, passed4 = m.sem("passed3"), m.sem("passed4")
        mixed = m.sem("mixed")

        block = ctx.enter_context(nc.Block())

        def rolled(eng, chunk):
            def turn(i, cs):
                for c in cs:
                    chunk(PER * i + c, i, c)
            turn(-1, (PER - 3, PER - 2, PER - 1))
            turn(0, range(PER))
            with eng.Fori(1, CHUNKS // PER - 1) as i:
                turn(i, range(PER))
            turn(CHUNKS // PER - 1, range(PER))
            turn(CHUNKS // PER, (0, 1))

        def group(i, c):
            return PER // 2 * i + c // 2

        def ahead(i, c, n):
            return i + (c + n) // PER, (c + n) % PER

        def adds(i, c, n):
            return PER // 2 * sum(ADDS) * i + sum(ADDS) * (c // 2) + ADDS[0] * (c % 2) + AFTER[c % 2][n]

        @block.sync
        def _(sp):
            def load_q(pair, n):
                at = slice(CH * n, CH * (n + 1))
                for u in range(2):
                    src = qk_scratch[pair][DH * u:DH * (u + 1), :, at]
                    for dst, kind in ((q_hh[u][0:DH, at], 0), (q_hh[u][DH:P, at], 0), (q_lm[u][0:DH, at], 1)):
                        sp.dma_start(dst.bitcast(F32), src[:, kind, :]).then_inc(q_in[n], 16)

            def load_k(pair, w):
                for u in range(2):
                    src = qk_scratch[pair][DH * u:DH * (u + 1), :, :]
                    for half in range(2):
                        sp.dma_start(k_hl[w][u][DH * half:DH * (half + 1), :].bitcast(F32), src[:, 2 + half, :]).then_inc(k_in[w], 16)

            def load_v(pair, w):
                b, pair_of_b = pair // (H // 2), pair % (H // 2)
                for u in range(2):
                    sp.dma_start(k_h1[w][u][0:DH, :].bitcast(F32), qk_scratch[pair][DH * u:DH * (u + 1), 2, :]).then_inc(v_in[w], 16)
                    for c in range(QC):
                        sp.dma_start(v_sb[w][u][:, CT * c:CT * (c + 1), :],
                                     v_scratch[QC * b + c][:, bass.ds(2 * pair_of_b + u, 1), :, :].rearrange("p h j d -> p (h j) d")
                                     ).then_inc(v_in[w], 16)

            load_q(0, 0)
            load_k(0, 0)
            load_q(0, 1)
            sp.dma_start(ident[:, :], identity).then_inc(consts_in, 16)
            sp.dma_start(mask_sb[DH:KM, :, :], row_mask.rearrange("m (t q) -> m t q", q=P)).then_inc(consts_in, 16)
            load_v(0, 0)
            sp.dma_start(w_out_sb[:, :, :], w_out.rearrange("(h p) n -> p h n", p=P)).then_inc(consts_in, 16)
            sp.dma_start(acc[:, :, :], acc_scratch).then_inc(acc_in, 16)
            for n in (2, 3):
                load_q(0, n)
            load_k(1, 1)
            load_v(1, 1)

            def turn(i, last):
                for w in range(2):
                    if last and w == 1:
                        return
                    for n in range(QC):
                        sp.wait_ge(s_done, 16 * (PER * i + 8 * w + 2 * n + 2))
                        sp.sem_inc(passed4, 1)
                        load_q(2 * i + w + 1, n)
                    if not last:
                        sp.wait_ge(pv_done, 8 * (PER * i + 8 * w + 8))
                        sp.sem_inc(passed4, 1)
                        load_k(2 * i + w + 2, w)
                        load_v(2 * i + w + 2, w)

            with sp.Fori(0, PAIRS // 2 - 1) as i:
                turn(i, False)
            turn(PAIRS // 2 - 1, True)
            out_t = out.rearrange("(t p) d -> p t d", p=P)
            for n in range(B * QC):
                last = GROUPS // B * (n // QC + 1) - QC + n % QC
                tiles = slice(CT * n, CT * (n + 1))
                sp.wait_ge(acc_done3, 2 * (last + 1))
                sp.wait_ge(mixed, CHOICES * CT * (n + 1))
                sp.dma_start(out_t[:, tiles, :], acc[:, tiles, :]).then_inc(out_done, 16)
            sp.wait_ge(out_done, 16 * B * QC)

        @block.tensor
        def _(pe):
            def scores_T(k, i, c, n):
                w, u, q = c // 8, n % 2, CH * (c // 2 % QC)
                tile = 8 * (c % 2) + n // 2
                keys = slice(P * tile, P * (tile + 1))
                if n == 0 and c % 8 == 0:
                    pe.wait_ge(v_in[w], V_LOAD * (i + 1))
                if n == 0 and c % 2 == 0:
                    pe.wait_ge(row_set, k + 2)
                need(pe, exp_done, 16 * k + n - 1)
                nc.tensor.matmul(s_bank[n % 2][:, :], k_hl[w][u][:, keys], q_hh[u][:, q:q + CH], start=True, stop=False)
                nc.tensor.matmul(s_bank[n % 2][:, :], k_h1[w][u][:, keys], q_lm[u][:, q:q + CH], start=False, stop=True
                                 ).then_inc(s_done, 1)

            def scores(k, i, c, n):
                i, c = ahead(i, c, 3)
                w, u, slot = c // 8, c % 2, c // 2 % QC
                q = CH * slot + P * (n // 4)
                if n == 0 and c % 8 == 0:
                    pe.wait_ge(k_in[w], K_LOAD * (i + 1))
                if n == 0 and c % 2 == 0:
                    pe.wait_ge(q_in[slot], Q_LOAD * (2 * i + w + 1))
                need(pe, max_done[n % 2], 8 * (k + 3) + n // 2)
                nc.tensor.matmul(a_bank[n % 2][:, :], q_hh[u][:, q:q + P], k_hl[w][u][:, CH * (n % 4):CH * (n % 4 + 1)],
                                 start=True, stop=True).then_inc(a_done, 1)

            def values(k, i, c, pair):
                if pair == 0 and c % 2 == 0:
                    need(pe, norm_done, group(i, c) - 1)
                pe.wait_ge(exp_done, 16 * k + 2 * pair + 2)
                for u in range(2):
                    mm = nc.tensor.matmul(o_bank[c // 2 % 2][DH * u:DH * (u + 1), :], v_sb[c // 8][u][:, 8 * (c % 2) + pair, :],
                                          probs[:, (2 * pair + u) % 8, :], start=(c % 2 == 0 and pair == 0),
                                          stop=(c % 2 == 1 and pair == 7))
                mm.then_inc(pv_done, 1)

            def output(k, i, c, half):
                i, c = ahead(i, c, -3)
                pair = (2 * i + c // 8) % (H // 2)
                pe.wait_ge(norm_done, group(i, c) + 1)
                need(pe, row_set, min(k + 3, CHUNKS) if isinstance(k, int) else k + 3)
                for t in range(2):
                    tile = slice(P * (2 * half + t), P * (2 * half + t + 1))
                    mm = nc.tensor.matmul(m_bank[half][:, D * t:D * (t + 1)], normed[c // 2 % 2][:, tile],
                                          w_out_sb[:, bass.ds(pair, 1), :].rearrange("p h n -> p (h n)"), start=True, stop=True)
                mm.then_inc(op_done, 1)

            def chunk(k, i, c):
                g = group(i, c)
                for pair in range(8):
                    for n in (2 * pair, 2 * pair + 1):
                        if within(k, CHUNKS):
                            scores_T(k, i, c, n)
                        if within(k + 3, CHUNKS):
                            scores(k, i, c, n)
                    if pair < 2 and within(k - 1, CHUNKS):
                        values(k - 1, *ahead(i, c, -1), pair + 6)
                    if pair >= 2 and within(k, CHUNKS):
                        values(k, i, c, pair - 2)
                    if pair in (3, 4) and c % 2 == 1 and within(g - 1, GROUPS):
                        output(k, i, c, pair - 3)
                    if pair == 3 and c % 2 == 0 and within(g - 1, GROUPS):
                        pe.wait_ge(add_done, sum(ADDS) * g)
                        need(pe, acc_done3, 2 * (g - 1))
                        for u in range(2):
                            mm = nc.tensor.matmul(m_bank[1][DH * u:DH * (u + 1), :], ones_sb[:, :], sums[(c // 2 - 1) % 2][:, u, :],
                                                  start=True, stop=True)
                        mm.then_inc(l_done, 1)
                    if pair == 0 and within(k + 2, CHUNKS):
                        if isinstance(k, int) and k == -2:
                            pe.wait_ge(consts_in, 48)
                            pe.wait_ge(consts_set, 6)
                            pe.wait_ge(blank_set, 3)
                        pe.wait_ge(negmax_set, k + 3)
                        need(pe, row_set, k + 2)
                        need(pe, acc_done3, 2 * (g - 2) + 1)
                        nc.tensor.transpose(m_bank[0][0:KM, 0:P], neg_max[c % 2][:, :], ident[:, :]).then_inc(row_done, 1)

            rolled(pe, chunk)

        @block.scalar
        def _(act):
            def chunk(k, i, c):
                for n in range(ST):
                    if within(k, CHUNKS):
                        if n % 2 == 0:
                            need(act, pv_done, 8 * k + n // 2 - 3)
                        if n % 2 == 0 and (n >= 8 or not isinstance(k, int) or k > 0):
                            before, pair = (k, n // 2 - 4) if n >= 8 else (k - 1, n // 2 + 4)
                            if pair in (2, 3):
                                act.wait_ge(pair_done, before + 1)
                            else:
                                act.wait_ge(add_done, adds(*(ahead(i, c, 0) if n >= 8 else ahead(i, c, -1)), pair))
                        act.wait_ge(s_done, 16 * k + n + 1)
                        nc.scalar.activation(probs[:, n % 8, :], s_bank[n % 2][:, :], ACT.Exp, scale=SCALE).then_inc(exp_done, 1)

            rolled(act, chunk)

        @block.vector
        def _(dve):
            for n in range(2):
                nc.vector.memset(neg_max[n][:, :], 0.0).then_inc(blank_set, 1)
            nc.vector.memset(ones_sb[:, :], 1.0).then_inc(blank_set, 1)
            dve.wait_ge(blank_set, 3)

            def add_output(k, i, c, half):
                g = group(i, c) - 1
                if isinstance(g, int) and g == 0:
                    dve.wait_ge(acc_in, 16)
                i1, c1 = ahead(i, c, -3)
                tile = TILES // B * (i1 // (PAIRS // B // 2)) + CT * (c1 // 2 % QC) + 2 * half
                at = acc[:, bass.ds(tile, 2), :]
                dve.wait_ge(op_done, 2 * g + half + 1)
                need(dve, acc_done3, 2 * g + half - 7)
                need(dve, mixed, g + 1)
                nc.vector.tensor_tensor(at, m_bank[half][:, :].rearrange("p (t n) -> p t n", n=D), at, ALU.add
                                        ).then_inc(acc_done3, 1)

            def chunk(k, i, c):
                g = group(i, c)
                for n in range(16):
                    if within(k + 3, CHUNKS):
                        dve.wait_ge(a_done, 16 * (k + 3) + n + 1)
                        nc.vector.tensor_reduce(maxes[(c + 1) % 2][:, n // 4, n % 4:n % 4 + 1], a_bank[n % 2][:, :], AX.X, ALU.max
                                                ).then_inc(max_done[n % 2], 1)
                    if n == 9 and within(k, CHUNKS):
                        dve.wait_ge(exp_done, 16 * k + 8)
                        if not isinstance(k, int) or k > 0:
                            dve.wait_ge(add_done, adds(*ahead(i, c, -1), 3))
                        nc.vector.tensor_tensor(pair_sum[:, :, :], probs[:, 4:6, :], probs[:, 6:8, :], ALU.add).then_inc(pair_done, 1)
                    if n == (3, 5)[c % 2] and within(k + 2, CHUNKS):
                        if isinstance(k, int) and k == -2:
                            dve.wait_ge(consts_in, 48)
                            dve.wait_ge(consts_set, 6)
                        q = CH * (ahead(i, c, 2)[1] // 2 % QC)
                        dve.wait_ge(row_done, k + 3)
                        nc.vector.tensor_tensor(q_lm[c % 2][DH:KM, q:q + CH].rearrange("m (t q) -> m t q", q=P),
                                                m_bank[0][DH:KM, 0:P].unsqueeze(1).broadcast_to([CT, CT, P]),
                                                mask_sb[DH:KM, :, :], ALU.mult).then_inc(row_set, 1)
                    if n in (11, 13) and c % 2 == 1 and within(g - 1, GROUPS):
                        add_output(k, i, c, (11, 13).index(n))
                    if n == (11, 1)[c % 2] or n in (13, 15) and c % 2 == 0:
                        part = 3 if c % 2 else (11, 13, 15).index(n)
                        if within(g - 1, GROUPS):
                            dve.wait_ge(l_done, g)
                            need(dve, norm_done, g - 1)
                            at = slice(P * part, P * (part + 1))
                            nc.vector.reciprocal(rsum[:, at], m_bank[1][:, at]).then_inc(rsum_set, 1)
                    if n == 3 and c % 2 == 1 and within(g - 1, GROUPS):
                        dve.wait_ge(rsum_set, 4 * g)
                        dve.wait_ge(pv_done, 16 * g)
                        need(dve, op_done, 2 * (g - 2))
                        v = (c // 2 - 1) % 2
                        nc.vector.tensor_tensor(normed[v][:, :], o_bank[v][:, :], rsum[:, :], ALU.mult).then_inc(norm_done, 1)
                    if n == 15 and c % 2 == 1 and within(k, CHUNKS):
                        choice, tile = c // 2 % 2, 4 * i + c // 4
                        if isinstance(k, int) and k == 1:
                            dve.wait_ge(acc_in, 16)
                        dve.wait_ge(fetched[choice], 16 * (tile + 1))
                        need(dve, acc_done3, 2 * g)
                        need(dve, mixed, g)
                        at = acc[:, bass.ds(tile, 1), :].rearrange("p t d -> p (t d)")
                        nc.vector.scalar_tensor_tensor(at, y_in[choice][:, :], weights[:, choice, bass.ds(tile, 1)], at, ALU.mult, ALU.add
                                                       ).then_inc(mixed, 1)
                if within(k + 3, CHUNKS):
                    for n in range(2):
                        dve.wait_ge(max_done[n], 8 * (k + 4))
                    need(dve, row_done, k + 2)
                    nc.vector.tensor_reduce(neg_max[(c + 1) % 2][:, DH:KM], maxes[(c + 1) % 2][:, :, :], AX.X, ALU.max, negate=True
                                            ).then_inc(negmax_set, 1)

            rolled(dve, chunk)

        @block.gpsimd
        def _(pool):
            def chunk(k, i, c):
                if not within(k, CHUNKS):
                    return
                g = group(i, c)
                if c % 2 == 0:
                    need(pool, l_done, g - 1)
                total = sums[c // 2 % 2]
                for pair in ((1, 3, 4, 5, 6, 7) if c % 2 == 0 else (0, 1, 3, 4, 5, 6, 7)):
                    if pair == 3:
                        pool.wait_ge(pair_done, k + 1)
                        term = pair_sum[:, :, :]
                    else:
                        pool.wait_ge(exp_done, 16 * k + 2 * pair + 2)
                        term = probs[:, 2 * (pair % 4):2 * (pair % 4) + 2, :]
                    first = c % 2 == 0 and pair == 1
                    need(pool, add_done, adds(i, c, pair) - 1)
                    nc.gpsimd.tensor_tensor(total[:, :, :], probs[:, 0:2, :] if first else total[:, :, :], term, ALU.add
                                            ).then_inc(add_done, 1)
                if c % 2 == 0:
                    n, tile = c // 2 % 2, 4 * i + c // 4
                    need(pool, mixed, g - 1)
                    need(pool, fetched[n], 16 * tile)
                    nc.gpsimd.tensor_copy(slot_now[n][:, :], slots[:, n, bass.ds(tile, 1)]).then_inc(slot_set, 1)
                    pool.wait_ge(slot_set, g + 1)
                    pool.sem_inc(passed3, 1)
                    nc.gpsimd.indirect_dma_start(y_in[n][:, :], None, y_rows, bass.IndirectOffsetOnAxis(ap=slot_now[n][:, :], axis=0)
                                                 ).then_inc(fetched[n], 16)

            for n in range(2):
                nc.gpsimd.memset(q_lm[n][DH:KM, :].bitcast(F32), 0.0).then_inc(consts_set, 1)
                for w in range(2):
                    nc.gpsimd.memset(k_h1[w][n][DH:KM, :].bitcast(F32), 1.0).then_inc(consts_set, 1)
            pool.wait_ge(consts_set, 6)
            rolled(pool, chunk)


def program(nc, x, wdq, wdkv, w_qk, wuv, w_out, ln_scale, ln_bias, router, w_gu, w_dn,
            identity, iota, earlier, iota_tiles, row_mask, cos_t, sin_t, out):
    def scratch(name, shape):
        return nc.dram_tensor(name, shape, F32).ap()

    v_scratch = scratch("v_scratch", (TOKENS // CH, P, H, CT, DH))
    qk_scratch = scratch("qk_scratch", (PAIRS, P, 4, S))
    xn_scratch = scratch("xn_scratch", (TOKENS // CH, CH, D))
    acc_scratch = scratch("acc_scratch", (P, TILES, D))
    slot_rows = scratch("slot_rows", (SLOT_TILES * P, D))
    y_rows = scratch("y_rows", (SLOT_TILES * P, D))
    with ExitStack() as ctx:
        slots = ctx.enter_context(nc.sbuf_tensor("slots", [P, CHOICES, TILES], U32))
        weights = ctx.enter_context(nc.sbuf_tensor("weights", [P, CHOICES, TILES], F32))
        with ExitStack() as inner:
            cT = inner.enter_context(nc.sbuf_tensor("cT", [P, 2, TOKENS], F32))
            tile_expert = inner.enter_context(nc.sbuf_tensor("tile_expert", [1, SLOT_TILES], mybir.dt.int32))
            phase_norm(nc, x, wdq, wdkv, wuv, router, ln_scale, ln_bias, identity, iota, earlier, iota_tiles,
                       v_scratch, xn_scratch, acc_scratch, slot_rows, cT, slots, weights, tile_expert)
            phase_experts(nc, w_gu, w_dn, w_qk, cos_t, sin_t, identity, xn_scratch, slot_rows, y_rows, qk_scratch,
                          cT, slots, tile_expert)
        phase_attention(nc, identity, row_mask, w_out, qk_scratch, v_scratch, acc_scratch, y_rows, slots, weights, out)


def rotary_tables():
    inv_freq = 1.0 / 10000.0 ** (np.arange(0, DH, 2, dtype=np.float32) / DH)
    freqs = np.outer(np.arange(S, dtype=np.float32), inv_freq)
    cos = np.concatenate([np.cos(freqs), np.cos(freqs)], -1)[:, ::2]
    sin = np.concatenate([np.sin(freqs), np.sin(freqs)], -1)[:, ::2]
    c, s = cos.T.astype(np.float32), sin.T.astype(np.float32)
    return np.concatenate([c, c, c, c]), np.concatenate([-s, s, -s, s])


def kernel(**inputs):
    import concourse.bacc as _bacc
    from concourse.bass_utils import run_bass_kernel_spmd as _run

    a = {n.removeprefix("L0_"): np.asarray(v) for n, v in inputs.items()}

    def rows_of_heads(w, flip):
        r = w.reshape(H // 2, 2, DH // 2, 2, LATENT)
        r = r[:, :, :, ::-1] if flip else r
        return r.transpose(0, 4, 1, 3, 2).reshape(H // 2, LATENT, P)

    up_q, up_k = a["attn_w_up_q"], a["attn_w_up_k"]
    cos_t, sin_t = rotary_tables()
    arrays = {
        "x": a["attn_x"].reshape(TOKENS, D),
        "wdq": a["attn_w_down_q"].T,
        "wdkv": a["attn_w_down_kv"].T,
        "w_qk": np.stack([rows_of_heads(w, f) for w in (up_q, up_k) for f in (False, True)], axis=2),
        "wuv": a["attn_w_up_v"].T,
        "w_out": a["attn_w_out"].T,
        "ln_scale": a["attn_ln_scale"].reshape(KD, P).T,
        "ln_bias": a["attn_ln_bias"].reshape(KD, P).T,
        "router": a["ffn_router_w"],
        "w_gu": a["ffn_w_gate_up"].reshape(E, KD, P, 2 * F).transpose(2, 0, 1, 3),
        "w_dn": a["ffn_w_down"].reshape(E, F // P, P, D).transpose(2, 0, 1, 3),
        "identity": np.eye(P, dtype=np.float32),
        "iota": np.tile(np.arange(E, dtype=np.float32), (P, 1)),
        "earlier": np.triu(np.ones((P, P), np.float32), 1),
        "iota_tiles": np.repeat(np.arange(SLOT_TILES, dtype=np.float32), E)[None],
        "row_mask": np.repeat(np.eye(CT, dtype=np.float32), P, axis=1),
        "cos_t": cos_t,
        "sin_t": sin_t,
    }
    nc = _bacc.Bacc("TRN2", target_bir_lowering=False, num_devices=1)
    feeds, args = {}, []
    for name, array in arrays.items():
        feeds[f"in_{name}"] = np.ascontiguousarray(array)
        args.append(nc.dram_tensor(f"in_{name}", array.shape, F32, kind="ExternalInput").ap())
    args.append(nc.dram_tensor("out_0", (TOKENS, D), F32, kind="ExternalOutput").ap())
    program(nc, *args)
    r = _run(nc, [feeds], core_ids=[0])
    return r.results[0]["out_0"].reshape(B, S, D)
```
